# Optimizing a Trainium2 kernel written in Bass

```python
import numpy as np
import jax
import jax.numpy as jnp

def _softmax(x, axis=-1):
    return jax.nn.softmax(x, axis=axis)

def _gelu(x):
    return jax.nn.gelu(x, approximate=True)

def _silu(x):
    return jax.nn.silu(x)

def _sigmoid(x):
    return jax.nn.sigmoid(x)

def _layernorm(x, axis=-1, eps=1e-05):
    m = jnp.mean(x, axis=axis, keepdims=True)
    v = jnp.var(x, axis=axis, keepdims=True)
    return (x - m) / jnp.sqrt(v + eps)

def _scatter_add(tgt, idx, src, axis=0):
    return tgt.at[idx].add(src)

def _segment_sum(src, seg, n):
    return jax.ops.segment_sum(src, seg, n)
kernel_name = 'mk_adaln_d1_jaxref_r8_6a608c'

def setup_inputs(seed: int=0):
    np.random.seed(seed)
    _w = jnp.asarray

    def _L0_attn_setup():
        import jax, jax.numpy as jnp
        import numpy as np
        N_EMBD = 128
        N_HEAD = 16
        HEAD_DIM = N_EMBD // N_HEAD
        LATENT_DIM = N_EMBD // 2
        B, T = (4, 256)
        key = jax.random.key(seed)
        ks = jax.random.split(key, 5)

        def init(k, fan_in, fan_out):
            bound = 1.0 / np.sqrt(fan_in)
            return jax.random.uniform(k, (fan_in, fan_out), jnp.float32, -bound, bound)
        return {'x': jax.random.normal(ks[0], (B, T, N_EMBD), jnp.float32), 'Wc_down': init(ks[1], N_EMBD, LATENT_DIM), 'Wq_up': init(ks[2], LATENT_DIM, N_EMBD), 'Wkv_up': init(ks[3], LATENT_DIM, 2 * HEAD_DIM), 'Wc_proj': init(ks[4], N_EMBD, N_EMBD)}
    _L0_attn_in = _L0_attn_setup()

    def _L0_ffn_setup():
        import jax, jax.numpy as jnp
        import numpy as np
        TEMPERATURE = 1.0
        NUM_EXPERTS = 8
        key = jax.random.key(seed)
        ks = jax.random.split(key, 7)
        B, S, H, E = (4, 512, 128, NUM_EXPERTS)
        scale = 1.0 / np.sqrt(H)
        return {'hidden_states': jax.random.normal(ks[0], (B, S, H), dtype=jnp.float32), 'w1': jax.random.normal(ks[1], (H, H // 2), dtype=jnp.float32) * scale, 'b1': jax.random.normal(ks[2], (H // 2,), dtype=jnp.float32) * 0.01, 'w2': jax.random.normal(ks[3], (H // 2, E), dtype=jnp.float32) * (1.0 / np.sqrt(H // 2)), 'b2': jax.random.normal(ks[4], (E,), dtype=jnp.float32) * 0.01, 'expert_W': jax.random.normal(ks[5], (E, H, H), dtype=jnp.float32) * scale, 'expert_b': jax.random.normal(ks[6], (E, H), dtype=jnp.float32) * 0.01}
    _L0_ffn_in = _L0_ffn_setup()
    _L0_c = _w((lambda *s: np.random.randn(*s).astype(np.float32) * 0.05)(32, 128))
    _L0_wmod = _w((lambda *s: np.random.randn(*s).astype(np.float32) * 0.05)(128, 6 * 128) * 128 ** (-0.5))
    _d = {'L0_attn_x': _L0_attn_in['x'], 'L0_attn_Wc_down': _L0_attn_in['Wc_down'], 'L0_attn_Wq_up': _L0_attn_in['Wq_up'], 'L0_attn_Wkv_up': _L0_attn_in['Wkv_up'], 'L0_attn_Wc_proj': _L0_attn_in['Wc_proj'], 'L0_ffn_w1': _L0_ffn_in['w1'], 'L0_ffn_b1': _L0_ffn_in['b1'], 'L0_ffn_w2': _L0_ffn_in['w2'], 'L0_ffn_b2': _L0_ffn_in['b2'], 'L0_ffn_expert_W': _L0_ffn_in['expert_W'], 'L0_ffn_expert_b': _L0_ffn_in['expert_b'], 'L0_c': _L0_c, 'L0_wmod': _L0_wmod}
    _x0 = _d['L0_attn_x']
    _d['L0_attn_x'] = jax.random.normal(jax.random.fold_in(jax.random.key(seed), 1), (32, 256, 128), dtype=_x0.dtype)
    del _x0
    return _d

def reference(L0_attn_x, L0_attn_Wc_down, L0_attn_Wq_up, L0_attn_Wkv_up, L0_attn_Wc_proj, L0_ffn_w1, L0_ffn_b1, L0_ffn_w2, L0_ffn_b2, L0_ffn_expert_W, L0_ffn_expert_b, L0_c, L0_wmod):

    def _L0_attn_ref(x, Wc_down, Wq_up, Wkv_up, Wc_proj):
        import jax, jax.numpy as jnp
        import numpy as np
        N_EMBD = 128
        N_HEAD = 16
        HEAD_DIM = N_EMBD // N_HEAD
        LATENT_DIM = N_EMBD // 2
        B, T = (4, 256)
        Bsz, Tlen, C = x.shape
        latent = x @ Wc_down
        q = (latent @ Wq_up).reshape(Bsz, Tlen, N_HEAD, HEAD_DIM)
        kv = latent @ Wkv_up
        k, v = (kv[..., :HEAD_DIM], kv[..., HEAD_DIM:])
        scale = 1.0 / np.sqrt(HEAD_DIM)
        att = jnp.einsum('bthd,bsd->bhts', q, k) * scale
        causal = jnp.tril(jnp.ones((Tlen, Tlen), dtype=bool))
        att = jnp.where(causal[None, None], att, -jnp.inf)
        att = jax.nn.softmax(att, axis=-1)
        y = jnp.einsum('bhts,bsd->bthd', att, v).reshape(Bsz, Tlen, C)
        return y @ Wc_proj

    def _L0_ffn_ref(hidden_states, w1, b1, w2, b2, expert_W, expert_b):
        import jax, jax.numpy as jnp
        import numpy as np
        TEMPERATURE = 1.0
        NUM_EXPERTS = 8
        h = jax.nn.relu(jnp.einsum('bsh,hm->bsm', hidden_states, w1) + b1)
        routing_scores = (jnp.einsum('bsm,me->bse', h, w2) + b2) / TEMPERATURE
        expert_probs = jax.nn.softmax(routing_scores, axis=-1)
        top_idx = jnp.argmax(expert_probs, axis=-1)
        onehot = jax.nn.one_hot(top_idx, NUM_EXPERTS, dtype=hidden_states.dtype)
        routed = jnp.zeros_like(hidden_states)
        for e in range(NUM_EXPERTS):
            mask = onehot[..., e:e + 1]
            expert_out = jnp.einsum('bsh,hd->bsd', hidden_states * mask, expert_W[e]) + expert_b[e]
            routed = routed + expert_out * mask
        return routed
    x = L0_attn_x
    mod = (_silu(L0_c) @ L0_wmod).reshape(L0_c.shape[0], 6, 1, -1)
    sa, ca, ga, sb, cb, gb = (mod[:, 0], mod[:, 1], mod[:, 2], mod[:, 3], mod[:, 4], mod[:, 5])
    ga = (2 * (ga >= 0) - 1) * jnp.maximum(jnp.abs(ga), 0.25)
    gb = (2 * (gb >= 0) - 1) * jnp.maximum(jnp.abs(gb), 0.25)
    h = _layernorm(x, axis=-1) * (1 + ca) + sa
    x = x + ga * _L0_attn_ref(h, L0_attn_Wc_down, L0_attn_Wq_up, L0_attn_Wkv_up, L0_attn_Wc_proj)
    h = _layernorm(x, axis=-1) * (1 + cb) + sb
    x = x + gb * _L0_ffn_ref(h, L0_ffn_w1, L0_ffn_b1, L0_ffn_w2, L0_ffn_b2, L0_ffn_expert_W, L0_ffn_expert_b)
    return x

_drawn_inputs = setup_inputs


def setup_inputs(seed=0):
    import zlib

    import numpy as np

    out = dict(_drawn_inputs(seed))
    spreads = {}
    factors = {'L0_attn_Wc_down': 2.841,
     'L0_attn_Wq_up': 7.477,
     'L0_attn_Wkv_up': 2.863,
     'L0_attn_Wc_proj': 2.742,
     'L0_ffn_expert_b': 31.327,
     'L0_ffn_b1': 2.98}
    for name, (base, spread) in spreads.items():
        noise = np.random.default_rng([zlib.crc32(name.encode()), seed]).standard_normal(out[name].shape)
        drawn = base * np.exp(spread * noise) if base else spread * noise
        out[name] = jnp.asarray(drawn.astype(out[name].dtype))
    for name, factor in factors.items():
        out[name] = (out[name] * factor).astype(out[name].dtype)
    return out
```

```python
from contextlib import ExitStack

import concourse.bass as bass
from concourse import mybir

F32 = mybir.dt.float32
BF16 = mybir.dt.bfloat16
I32 = mybir.dt.int32
ALU = mybir.AluOpType
ACT = mybir.ActivationFunctionType
AX = mybir.AxisListType


class Batch:

    def __init__(self, pair, ahead, parity, n_batches):
        self.pair, self.ahead, self.parity, self.n_batches = pair, ahead, parity, n_batches

    def plus(self, n):
        whole = self.parity + n
        return Batch(self.pair, self.ahead + whole // 2, whole % 2, self.n_batches)

    @property
    def index(self):
        return self.pair * 2 + (2 * self.ahead + self.parity)

    @property
    def exists(self):
        return not isinstance(self.pair, int) or 0 <= self.index < self.n_batches

    def at_least(self, n):
        return not isinstance(self.pair, int) or self.index >= n

    def count(self, per_batch, k):
        return self.pair * (2 * per_batch) + ((2 * self.ahead + self.parity) * per_batch + k)

    def pair_count(self, per_batch, k):
        return self.pair * per_batch + (self.ahead * per_batch + k)


def adaln_block(nc, x, w_down, w_q, w_kv, w_proj, w1, b1, w2, b2, expert_w, expert_b, cond, w_mod, out,
                q_scratch, gate_scratch):
    NB, T, C = x.shape
    P = 128
    NT = T // P
    LAT = w_down.shape[1]
    HD = w_kv.shape[1] // 2
    NH = C // HD
    NE = expert_w.shape[0]
    HID = w1.shape[1]
    EPS = 1e-5
    SCALE = HD ** -0.5
    NEG = -1e30
    NC = NH // 4
    CH = 3 * NC
    PARTS = 3
    QR = PARTS * HD
    KR = 96
    KRS = KR + PARTS
    W = 512
    VW = 32
    EB = W // C
    MAX_CHUNKS = [2, 2, 1, 2, 1, 2, 1, 1, 0, 0, 0, 0]
    MAX_FROM = [sum(MAX_CHUNKS[:s]) for s in range(CH)]

    ctx = ExitStack()
    with ctx:
        def sb(name, shape, dt=F32):
            return ctx.enter_context(nc.sbuf_tensor(name, shape, dt))

        def two(name, shape, dt=F32):
            return [sb(f"{name}{i}", shape, dt) for i in range(2)]

        def sem(name):
            return ctx.enter_context(nc.semaphore(name))

        ident = sb("ident", [P, P])
        ident_b = sb("ident_b", [P, P], BF16)
        future = sb("future", [P, P], BF16)
        later = sb("later", [P, P], BF16)
        minus_half = sb("minus_half", [P, NT])
        rank = sb("rank", [P, NE])
        pick3 = sb("pick3", [P, P], BF16)
        wd_sb = sb("wd_sb", [C, LAT])
        wq_sb = sb("wq_sb", [LAT, C])
        wkv_sb = sb("wkv_sb", [LAT, 2 * HD])
        wk_rep = sb("wk_rep", [LAT, KR])
        wp_sb = sb("wp_sb", [C, C])
        w1_sb = sb("w1_sb", [C, HID])
        b1_sb = sb("b1_sb", [HID, 1])
        w2_sb = sb("w2_sb", [HID + 1, NE])
        we_sb = sb("we_sb", [C, NE * C])
        be_rows = sb("be_rows", [PARTS, NE * C])
        be_hi = sb("be_hi", [PARTS, NE * C], BF16)
        be_rest = sb("be_rest", [PARTS, NE * C])
        be_mid = sb("be_mid", [PARTS, NE * C], BF16)
        be_acc = sb("be_acc", [PARTS, NE * C])
        be_parts = sb("be_parts", [P, NE * C], BF16)
        c_sb = sb("c_sb", [NB, C])
        c_exp = sb("c_exp", [NB, C])
        c_silu = sb("c_silu", [NB, C])
        c_siluT = sb("c_siluT", [C, NB])
        wm_sb = sb("wm_sb", [C, 6 * C])
        mod = sb("mod", [C, 4, NB])
        g_sign = sb("g_sign", [NB, 2, C])
        g_raw = sb("g_raw", [NB, 2, C])
        g_size = sb("g_size", [NB, 2, C])

        x_in = two("x_in", [P, NT, C])
        x_res = two("x_res", [P, NT, C])
        gates = two("gates", [P, 2, C])
        stats = two("stats", [P, NT, 6])
        mean_var = two("mean_var", [P, NT, 2])
        var_eps = two("var_eps", [P, NT])
        rstd = two("rstd", [P, NT])
        xn = two("xn", [P, NT, C])
        hT = two("hT", [C, T])
        latT = two("latT", [LAT, T])
        q_parts = two("q_parts", [C, PARTS, T], BF16)
        q_rest = two("q_rest", [C, T])
        k_rest = two("k_rest", [KR, T])
        k_mid = two("k_mid", [KR, T], BF16)
        k_new = two("k_new", [KR, T], BF16)
        k_cur = two("k_cur", [P, T], BF16)
        v_new = two("v_new", [P, NT, HD])
        v_cur = two("v_cur", [P, NT, VW])
        q_rows = two("q_rows", [P, NH, T], BF16)
        maxes = two("maxes", [P, NH, NT])
        max_rest = two("max_rest", [P, NH, NT])
        max_parts = two("max_parts", [P, PARTS, NH, NT], BF16)
        maxT = two("maxT", [PARTS * NH * NT, P], BF16)
        probs = [sb(f"probs{i}", [P, W]) for i in range(6)]
        y_raw = two("y_raw", [P, NC, T])
        r_den = two("r_den", [P, NT, NH])
        y_tok = two("y_tok", [P, NT, C])
        yT = two("yT", [C, T])
        x_gated = two("x_gated", [P, NT, C])
        x_mid = two("x_mid", [P, NT, C])
        stats2 = two("stats2", [P, NT, 6])
        mean_var2 = two("mean_var2", [P, NT, 2])
        var_eps2 = two("var_eps2", [P, NT])
        rstd2 = two("rstd2", [P, NT])
        xn2 = two("xn2", [P, NT, C])
        h2T = two("h2T", [C, T])
        hidT = two("hidT", [HID + 1, T])
        top = two("top", [P, NT])
        is_top = two("is_top", [P, NT, NE])
        top_rank = two("top_rank", [P, NT])
        ranked = two("ranked", [P, NT, NE])
        onehot = two("onehot", [P, NT, NE])
        chosen = two("chosen", [P, NT, NE, C])
        routed_g = two("routed_g", [P, NT, C])
        x_out = two("x_out", [P, NT, C])

        def bank(name):
            return ctx.enter_context(nc.psum_tensor(name, [P, W], F32))
        ps_s = [bank(f"ps_s{i}") for i in range(3)]
        ps_m = [bank(f"ps_m{i}") for i in range(2)]
        ps_y = bank("ps_y")
        ps_a = bank("ps_a")
        ps_b = bank("ps_b")

        weights_in = sem("weights_in")
        consts_made = sem("consts_made")
        gps_step = sem("gps_step")
        setup_act = sem("setup_act")
        setup_dve = sem("setup_dve")
        setup_pe = sem("setup_pe")
        setup_ready = sem("setup_ready")
        gates_out = sem("gates_out")
        x_in_loaded = [sem(f"x_in_loaded{i}") for i in range(2)]
        x_res_loaded = [sem(f"x_res_loaded{i}") for i in range(2)]
        q_written = [sem(f"q_written{i}") for i in range(2)]
        q_loaded = [[sem(f"q_loaded{i}_{c}") for c in range(NC)] for i in range(2)]
        shift_loaded = [sem(f"shift_loaded{i}") for i in range(2)]
        out_stored = [sem(f"out_stored{i}") for i in range(2)]
        ln1_dve = sem("ln1_dve")
        ln1_rstd = sem("ln1_rstd")
        xnT_done = sem("xnT_done")
        hT_ready = sem("hT_ready")
        lat_done = sem("lat_done")
        latT_ready = sem("latT_ready")
        qk_done = sem("qk_done")
        qk_high = sem("qk_high")
        qk_dve = sem("qk_dve")
        q_low = sem("q_low")
        v_done = sem("v_done")
        v_ready = sem("v_ready")
        max_scores = sem("max_scores")
        max_taken = sem("max_taken")
        max_split = sem("max_split")
        kv_moved = sem("kv_moved")
        maxT_done = sem("maxT_done")
        maxT_ready = sem("maxT_ready")
        scores_done = sem("scores_done")
        probs_ready = sem("probs_ready")
        pv_done = sem("pv_done")
        y_copied = sem("y_copied")
        y_turned = sem("y_turned")
        den_ready = sem("den_ready")
        y_normed = sem("y_normed")
        yT_done = sem("yT_done")
        yT_ready = sem("yT_ready")
        proj_done = sem("proj_done")
        x_mid_dve = sem("x_mid_dve")
        ln2_dve = sem("ln2_dve")
        ln2_rstd = sem("ln2_rstd")
        xn2T_done = sem("xn2T_done")
        h2T_ready = sem("h2T_ready")
        hid_done = sem("hid_done")
        hidT_ready = sem("hidT_ready")
        logits_done = sem("logits_done")
        route_dve = sem("route_dve")
        experts_done = sem("experts_done")
        expert_taken = sem("expert_taken")
        routed_gps = sem("routed_gps")
        out_ready = sem("out_ready")

        sp_went_on = sem("sp_went_on")
        dve_went_on = sem("dve_went_on")

        def steps(engine, step):
            first_pair, last_pair = 1, (NB - 4) // 2
            for i in range(-2, 2 * first_pair):
                step(Batch(0, i // 2, i % 2, NB))
            with engine.Fori(first_pair, last_pair) as pair:
                step(Batch(pair, 0, 0, NB))
                step(Batch(pair, 0, 1, NB))
            for i in range(2 * last_pair, NB + 2):
                step(Batch(0, i // 2, i % 2, NB))

        def score_chunk(c, kind):
            return (NC * c + 2 * kind, 2) if kind < 2 else (NC * c, 4)

        block = ctx.enter_context(nc.Block())

        @block.sync
        def _(sp):
            loads = [
                (c_sb[:, :], cond), (wm_sb[:, :], w_mod), (wd_sb[:, :], w_down), (wq_sb[:, :], w_q),
                (wkv_sb[:, :], w_kv), (wp_sb[:, :], w_proj), (w1_sb[:, :], w1),
                (b1_sb[:, :], b1.rearrange("(m a) -> m a", a=1)), (w2_sb[0:HID, :], w2),
                (w2_sb[HID:HID + 1, :], b2.rearrange("(a e) -> a e", a=1)),
                (we_sb[:, :].rearrange("h (e d) -> h e d", e=NE), expert_w.rearrange("e h d -> h e d")),
            ] + [(be_rows[p:p + 1, :], expert_b.rearrange("(a e) d -> a (e d)", a=1)) for p in range(PARTS)]
            assert len(loads) == 14
            for dst, src in loads:
                sp.dma_start(dst, src).then_inc(weights_in, 16)
            sp.wait_ge(setup_dve, 16)
            sp.dma_start(gate_scratch, g_size[:, :, :]).then_inc(gates_out, 16)
            sp.wait_ge(gates_out, 16)

            def load_x(b):
                src = x[bass.ds(b.index, 1), :, :].rearrange("a (n p) c -> p (a n) c", p=P)
                if b.at_least(2):
                    sp.wait_ge(ln1_dve, b.plus(-2).count(7, 7))
                    sp.sem_inc(sp_went_on, 1)
                sp.dma_start(x_in[b.parity][:, :, :], src).then_inc(x_in_loaded[b.parity], 16)

            def step(i):
                fill, soft, done = i.plus(2), i, i.plus(-2)
                if i.plus(3).exists and not (isinstance(i.pair, int) and i.index == -2):
                    load_x(i.plus(3))
                if done.exists:
                    sp.wait_ge(out_ready, done.count(1, 1))
                    sp.sem_inc(sp_went_on, 1)
                    sp.dma_start(out[bass.ds(done.index, 1), :, :].rearrange("a (n p) c -> p (a n) c", p=P),
                                 x_out[done.parity][:, :, :]).then_inc(out_stored[done.parity], 16)
                if soft.exists:
                    sp.dma_start(x_res[soft.parity][:, :, :],
                                 x[bass.ds(soft.index, 1), :, :].rearrange("a (n p) c -> p (a n) c", p=P)
                                 ).then_inc(x_res_loaded[soft.parity], 16)
                    sp.dma_start(gates[soft.parity][:, :, :],
                                 gate_scratch[bass.ds(soft.index, 1), :, :].broadcast_to([P, 2, C])
                                 ).then_inc(x_res_loaded[soft.parity], 16)
                if fill.exists:
                    sp.wait_ge(qk_dve, fill.count(6, 6))
                    sp.sem_inc(sp_went_on, 1)
                    sp.wait_ge(q_low, fill.count(1, 1))
                    if fill.at_least(2):
                        for c in range(NC):
                            sp.wait_ge(q_loaded[fill.parity][c], fill.plus(-2).pair_count(48, 48))
                    for pq in range(PARTS):
                        sp.dma_start(
                            q_scratch[fill.parity, pq * HD:(pq + 1) * HD, :, :].rearrange("d h t -> h d t"),
                            q_parts[fill.parity][:, pq, :]).then_inc(q_written[fill.parity], 16)
                    sp.wait_ge(q_written[fill.parity], fill.pair_count(48, 48))
                    sp.sem_inc(sp_went_on, 1)
                    for c in range(NC):
                        if soft.exists:
                            sp.wait_ge(scores_done, soft.count(CH, 3 * c + 3))
                        for pk in range(PARTS):
                            sp.dma_start(q_rows[fill.parity][32 * pk:32 * pk + QR, 4 * c:4 * c + 4, :],
                                         q_scratch[fill.parity, :, 4 * c:4 * c + 4, :]
                                         ).then_inc(q_loaded[fill.parity][c], 16)

            sp.wait_ge(setup_ready, 1)
            load_x(Batch(0, 0, 0, NB))
            load_x(Batch(0, 0, 1, NB))
            steps(sp, step)
            for par in range(2):
                sp.wait_ge(out_stored[par], 16 * NB // 2)

        @block.gpsimd
        def _(gp):
            k = [0]

            def made(ins):
                k[0] += 1
                ins.then_inc(gps_step, 1)
                gp.wait_ge(gps_step, k[0])

            made(gp.memset(ident[:, :], 0.0))
            made(gp.memset(future[:, :], 0.0))
            made(gp.memset(later[:, :], 0.0))
            made(gp.memset(pick3[:, :], 0.0))
            made(gp.memset(be_parts[:, :], 0.0))
            made(gp.memset(minus_half[:, :], -0.5))
            for e in range(NE):
                made(gp.memset(rank[:, e:e + 1], float(NE - e)))
            for par in range(2):
                made(gp.memset(q_rows[par][:, :, :], 0.0))
                made(gp.memset(v_cur[par][:, :, :], 0.0))
                made(gp.memset(k_cur[par][KR:KR + 32, :], -1.0))
                made(gp.memset(hidT[par][HID:HID + 1, :], 1.0))
            made(gp.memset(wk_rep[:, :], 0.0))
            made(gp.affine_select(out=ident[:, :], in_=ident[:, :], compare_op=ALU.not_equal, fill=1.0, base=0,
                                  pattern=[[-1, P]], channel_multiplier=1))
            made(gp.affine_select(out=future[:, :], in_=future[:, :], compare_op=ALU.is_ge, fill=NEG, base=0,
                                  pattern=[[-1, P]], channel_multiplier=1))
            made(gp.affine_select(out=later[:, :], in_=later[:, :], compare_op=ALU.is_ge, fill=NEG, base=0,
                                  pattern=[[1, P]], channel_multiplier=-1))
            made(gp.memset(pick3[0:PARTS, :], 1.0))
            for par in range(2):
                made(gp.memset(v_cur[par][:, :, HD:HD + 1], 1.0))
            gp.tensor_copy(ident_b[:, :], ident[:, :]).then_inc(consts_made, 1)

            def power(dst, src):
                return gp.tensor_tensor(dst, src, minus_half[:, :], ALU.pow)

            def step(i):
                fill, soft, end, done = i.plus(2), i, i.plus(-1), i.plus(-2)
                for s in range(CH):
                    if s == 0 and fill.exists:
                        gp.wait_ge(ln1_dve, fill.count(7, 5))
                        power(rstd[fill.parity][:, :], var_eps[fill.parity][:, :]).then_inc(ln1_rstd, 1)
                    if s == 2 and done.exists:
                        gp.wait_ge(expert_taken, done.count(2 * NT, 2 * NT))
                        ch = chosen[done.parity]
                        half, k = NE // 2, 0
                        while half:
                            gp.tensor_tensor(ch[:, :, 0:half, :], ch[:, :, 0:half, :], ch[:, :, half:2 * half, :],
                                             ALU.add).then_inc(routed_gps, 1)
                            half, k = half // 2, k + 1
                            gp.wait_ge(routed_gps, done.count(4, k))
                        gp.tensor_tensor(routed_g[done.parity][:, :, :], ch[:, :, 0, :],
                                         gates[done.parity][:, 1:2, :].broadcast_to([P, NT, C]), ALU.mult
                                         ).then_inc(routed_gps, 1)
                        gp.wait_ge(routed_gps, done.count(4, 4))
                        if done.at_least(2):
                            gp.wait_ge(out_stored[done.parity], done.plus(-2).pair_count(16, 16))
                        gp.tensor_tensor(x_out[done.parity][:, :, :], routed_g[done.parity][:, :, :],
                                         x_mid[done.parity][:, :, :], ALU.add).then_inc(out_ready, 1)
                    if s == 7 and end.exists:
                        gp.wait_ge(ln2_dve, end.count(7, 5))
                        power(rstd2[end.parity][:, :], var_eps2[end.parity][:, :]).then_inc(ln2_rstd, 1)
                    if s == 7 and fill.exists:
                        gp.wait_ge(qk_dve, fill.count(6, 3))
                        gp.tensor_tensor(q_parts[fill.parity][:, 2, :], q_rest[fill.parity][:, :],
                                         q_parts[fill.parity][:, 1, :], ALU.subtract).then_inc(q_low, 1)

            gp.wait_ge(setup_ready, 1)
            steps(gp, step)

        @block.scalar
        def _(act):
            act.wait_ge(weights_in, 16 * 14)
            nc.scalar.activation(c_exp[:, :], c_sb[:, :], ACT.Exp, scale=-1.0).then_inc(setup_act, 1)
            act.wait_ge(setup_ready, 1)

            def step(i):
                fill, maxi, soft, end = i.plus(2), i.plus(1), i, i.plus(-1)
                for s in range(CH):
                    if soft.exists:
                        act.wait_ge(scores_done, soft.count(CH, s + 1))
                        if s >= 6 or soft.at_least(1):
                            act.wait_ge(pv_done, soft.count(NC, s // 3 - 1))
                        nc.scalar.activation(probs[s % 6][:, :], ps_s[s % 3][:, :], ACT.Exp,
                                             scale=SCALE).then_inc(probs_ready, 1)
                    if s == 2 and fill.exists:
                        act.wait_ge(xnT_done, fill.count(1, 1))
                        nc.scalar.activation(hT[fill.parity][:, :], ps_a[:, 0:T], ACT.Identity,
                                             bias=mod[:, 0, bass.ds(fill.index, 1)],
                                             scale=mod[:, 1, bass.ds(fill.index, 1)]).then_inc(hT_ready, 1)
                    if s == 2 and end.exists:
                        act.wait_ge(pv_done, end.count(NC, NC))
                        nc.scalar.activation(y_raw[end.parity][:, 2:4, :],
                                             ps_y[:, :].rearrange("p (c t) -> p c t", c=2), ACT.Copy
                                             ).then_inc(y_copied, 1)
                    if s == 4 and fill.exists:
                        act.wait_ge(lat_done, fill.count(1, 1))
                        nc.scalar.activation(latT[fill.parity][:, :], ps_a[0:LAT, 0:T], ACT.Copy
                                             ).then_inc(latT_ready, 1)
                    if s == 6 and fill.exists:
                        act.wait_ge(qk_done, fill.count(1, 1))
                        if fill.at_least(2):
                            act.wait_ge(q_written[fill.parity], fill.plus(-2).pair_count(48, 48))
                        nc.scalar.activation(q_parts[fill.parity][:, 0, :], ps_a[:, 0:T], ACT.Copy
                                             ).then_inc(qk_high, 1)
                        nc.scalar.activation(k_new[fill.parity][:, :], ps_a[0:KR, T:2 * T], ACT.Copy
                                             ).then_inc(qk_high, 1)
                    if s == 6 and end.exists:
                        act.wait_ge(yT_done, end.count(1, 1))
                        nc.scalar.activation(yT[end.parity][:, :], ps_b[:, 0:T], ACT.Copy).then_inc(yT_ready, 1)
                    if s == 8 and fill.exists:
                        act.wait_ge(v_done, fill.count(1, 1))
                        nc.scalar.activation(v_new[fill.parity][:, :, :],
                                             ps_a[:, 0:NT * HD].rearrange("p (n d) -> p n d", n=NT), ACT.Copy
                                             ).then_inc(v_ready, 1)
                    if s == 8 and soft.exists:
                        act.wait_ge(pv_done, soft.count(NC, 2))
                        nc.scalar.activation(y_raw[soft.parity][:, 0:2, :],
                                             ps_y[:, :].rearrange("p (c t) -> p c t", c=2), ACT.Copy
                                             ).then_inc(y_copied, 1)
                    if s == 9 and maxi.exists:
                        act.wait_ge(maxT_done, maxi.count(1, 1))
                        nc.scalar.activation(maxT[maxi.parity][:, :],
                                             ps_a[0:PARTS * NH * NT, 0:P // 2].bitcast(BF16), ACT.Copy
                                             ).then_inc(maxT_ready, 1)
                    if s == 9 and end.exists:
                        act.wait_ge(xn2T_done, end.count(1, 1))
                        nc.scalar.activation(h2T[end.parity][:, :], ps_b[:, 0:T], ACT.Identity,
                                             bias=mod[:, 2, bass.ds(end.index, 1)],
                                             scale=mod[:, 3, bass.ds(end.index, 1)]).then_inc(h2T_ready, 1)
                    if s == 10 and maxi.exists:
                        act.wait_ge(maxT_ready, maxi.count(1, 1))
                        for p in range(PARTS):
                            act.dma_start(
                                q_rows[maxi.parity][KR + p:KR + p + 1, :, :].rearrange(
                                    "a h (n t) -> a (h n) t", n=NT),
                                maxT[maxi.parity][NH * NT * p:NH * NT * (p + 1), :]
                            ).then_inc(shift_loaded[maxi.parity], 16)
                    if s == 10 and end.exists:
                        act.wait_ge(hid_done, end.count(1, 1))
                        nc.scalar.activation(hidT[end.parity][0:HID, :], ps_b[0:HID, 0:T], ACT.Relu,
                                             bias=b1_sb[:, :]).then_inc(hidT_ready, 1)

            steps(act, step)

        @block.vector
        def _(dve):
            n = [0]

            def then(ins):
                n[0] += 1
                ins.then_inc(setup_dve, 1)
                dve.wait_ge(setup_dve, n[0])

            V = nc.vector
            dve.wait_ge(setup_act, 1)
            then(V.tensor_scalar(c_exp[:, :], c_exp[:, :], 1.0, None, ALU.add))
            then(V.reciprocal(c_exp[:, :], c_exp[:, :]))
            then(V.tensor_tensor(c_silu[:, :], c_sb[:, :], c_exp[:, :], ALU.mult))
            dve.wait_ge(setup_pe, 1)
            then(V.tensor_copy(c_siluT[:, :], ps_a[:, 0:NB]))
            dve.wait_ge(consts_made, 1)
            then(V.tensor_copy(be_hi[:, :], be_rows[:, :]))
            then(V.tensor_tensor(be_rest[:, :], be_rows[:, :], be_hi[:, :], ALU.subtract))
            then(V.tensor_copy(be_mid[:, :], be_rest[:, :]))
            then(V.tensor_tensor(be_rest[:, :], be_rest[:, :], be_mid[:, :], ALU.subtract))
            then(V.tensor_scalar(be_acc[:, :], be_hi[:, :], ident[0:PARTS, 0:1], None, ALU.mult))
            then(V.scalar_tensor_tensor(be_acc[:, :], be_mid[:, :], ident[0:PARTS, 1:2], be_acc[:, :],
                                        ALU.mult, ALU.add))
            then(V.scalar_tensor_tensor(be_parts[0:PARTS, :], be_rest[:, :], ident[0:PARTS, 2:3], be_acc[:, :],
                                        ALU.mult, ALU.add))
            dve.wait_ge(setup_pe, 2)
            gv = ps_b[0:NB, 0:2 * C].rearrange("b (g c) -> b g c", g=2)
            then(V.tensor_scalar(g_sign[:, :, :], gv, 0.0, 2.0, ALU.is_ge, ALU.mult))
            then(V.tensor_copy(g_raw[:, :, :], gv))
            then(V.scalar_tensor_tensor(g_size[:, :, :], g_raw[:, :, :], -1.0, g_raw[:, :, :], ALU.mult, ALU.max))
            then(V.tensor_scalar(g_size[:, :, :], g_size[:, :, :], 0.25, None, ALU.max))
            then(V.scalar_tensor_tensor(g_size[:, :, :], g_sign[:, :, :], -1.0, g_size[:, :, :],
                                        ALU.add, ALU.mult))
            for m in range(4):
                then(V.tensor_scalar(mod[:, m, :], ps_a[:, 64 * m:64 * m + NB], float(m % 2), None, ALU.add))
            for pk in range(PARTS):
                for pq in range(PARTS):
                    at = 32 * pk + HD * pq
                    then(V.tensor_copy(wk_rep[:, at:at + HD], wkv_sb[:, 0:HD]))
            V.memset(top[0][:, :], 0.0).then_inc(setup_ready, 1)

            def norm_stats(src, st, mv, ve, done, b):
                for t in range(NT):
                    V.bn_stats(st[:, t, :], src[:, t, :]).then_inc(done, 1)
                dve.wait_ge(done, b.count(7, 2))
                dve.sem_inc(dve_went_on, 1)
                for t in range(NT):
                    V.bn_aggr(mv[:, t, :], st[:, t, :]).then_inc(done, 1)
                dve.wait_ge(done, b.count(7, 4))
                V.tensor_scalar(ve[:, :], mv[:, :, 1], EPS, None, ALU.add).then_inc(done, 1)

            def norm_apply(dst, src, mv, rs, done):
                for t in range(NT):
                    V.tensor_scalar(dst[:, t, :], src[:, t, :], mv[:, t, 0:1], rs[:, t:t + 1],
                                    ALU.subtract, ALU.mult).then_inc(done, 1)

            def take_max(b, m):
                c, kind = m // 3, m % 3
                h0, heads = score_chunk(c, kind)
                dve.wait_ge(max_scores, b.count(CH, m + 1))
                V.tensor_reduce(maxes[b.parity][:, h0:h0 + heads, 1 if kind < 2 else 0],
                                ps_m[m % 2][:, :].rearrange("p (h s) -> p h s", h=heads),
                                AX.X, ALU.max).then_inc(max_taken, 1)

            def take_expert(b, t, half, bk):
                dve.wait_ge(experts_done, b.count(2 * NT, 2 * t + half + 1))
                if t + half == 0:
                    dve.wait_ge(route_dve, b.count(5, 5))
                V.tensor_tensor(chosen[b.parity][:, t, half * EB:(half + 1) * EB, :],
                                bk[:, :].rearrange("p (e c) -> p e c", e=EB),
                                onehot[b.parity][:, t, half * EB:(half + 1) * EB].unsqueeze(2).broadcast_to(
                                    [P, EB, C]), ALU.mult).then_inc(expert_taken, 1)

            def step(i):
                fill, maxi, soft, end, done = i.plus(2), i.plus(1), i, i.plus(-1), i.plus(-2)
                for s in range(CH):
                    if s == 0 and fill.exists:
                        dve.wait_ge(x_in_loaded[fill.parity], fill.pair_count(16, 16))
                        norm_stats(x_in[fill.parity], stats[fill.parity], mean_var[fill.parity],
                                   var_eps[fill.parity], ln1_dve, fill)
                    if s < NT and done.exists:
                        for half in range(2):
                            take_expert(done, s, half, (ps_a, ps_b)[half])
                    if maxi.exists:
                        for m in range(MAX_FROM[s], MAX_FROM[s] + MAX_CHUNKS[s]):
                            take_max(maxi, m)
                    if s == 1 and fill.exists:
                        dve.wait_ge(ln1_rstd, fill.count(1, 1))
                        norm_apply(xn[fill.parity], x_in[fill.parity], mean_var[fill.parity],
                                   rstd[fill.parity], ln1_dve)
                    if s in (3, 5) and end.exists:
                        t = (s - 3) // 2
                        dve.wait_ge(y_turned, end.count(NT, t + 1))
                        turned = ps_b[:, :].rearrange("p (h w) -> p h w", w=VW)
                        V.reciprocal(r_den[end.parity][:, t, :], turned[:, :, HD]).then_inc(den_ready, 1)
                        dve.wait_ge(den_ready, end.count(NT, t + 1))
                        V.tensor_tensor(y_tok[end.parity][:, t, :].rearrange("p (h d) -> p h d", d=HD),
                                        turned[:, :, 0:HD],
                                        r_den[end.parity][:, t, :].unsqueeze(2).broadcast_to([P, NH, HD]),
                                        ALU.mult).then_inc(y_normed, 1)
                    if s == 6 and fill.exists:
                        par = fill.parity
                        dve.wait_ge(qk_high, fill.count(2, 2))
                        V.tensor_tensor(q_rest[par][:, :], ps_a[:, 0:T], q_parts[par][:, 0, :],
                                        ALU.subtract).then_inc(qk_dve, 1)
                        V.tensor_tensor(k_rest[par][:, :], ps_a[0:KR, T:2 * T], k_new[par][:, :],
                                        ALU.subtract).then_inc(qk_dve, 1)
                        dve.wait_ge(qk_dve, fill.count(6, 2))
                        V.tensor_copy(q_parts[par][:, 1, :], q_rest[par][:, :]).then_inc(qk_dve, 1)
                        V.tensor_copy(k_mid[par][64:96, :], k_rest[par][64:96, :]).then_inc(qk_dve, 1)
                        V.tensor_copy(k_new[par][32:64, :], k_rest[par][32:64, :]).then_inc(qk_dve, 1)
                        dve.wait_ge(qk_dve, fill.count(6, 4))
                        V.tensor_tensor(k_new[par][64:96, :], k_rest[par][64:96, :], k_mid[par][64:96, :],
                                        ALU.subtract).then_inc(qk_dve, 1)
                    if s == 7 and end.exists:
                        par = end.parity
                        dve.wait_ge(proj_done, end.count(1, 1))
                        dve.wait_ge(x_res_loaded[par], end.pair_count(32, 32))
                        V.tensor_tensor(x_gated[par][:, :, :], ps_b[:, 0:T].rearrange("p (n c) -> p n c", n=NT),
                                        gates[par][:, 0:1, :].broadcast_to([P, NT, C]), ALU.mult
                                        ).then_inc(x_mid_dve, 1)
                        dve.wait_ge(x_mid_dve, end.count(2, 1))
                        V.tensor_tensor(x_mid[par][:, :, :], x_gated[par][:, :, :], x_res[par][:, :, :],
                                        ALU.add).then_inc(x_mid_dve, 1)
                        dve.wait_ge(x_mid_dve, end.count(2, 2))
                        norm_stats(x_mid[par], stats2[par], mean_var2[par], var_eps2[par], ln2_dve, end)
                    if s == 8 and maxi.exists:
                        par = maxi.parity
                        dve.wait_ge(max_taken, maxi.count(CH, CH))
                        V.tensor_copy(max_parts[par][:, 0, :, :], maxes[par][:, :, :]).then_inc(max_split, 1)
                        dve.wait_ge(max_split, maxi.count(4, 1))
                        V.tensor_tensor(max_rest[par][:, :, :], maxes[par][:, :, :], max_parts[par][:, 0, :, :],
                                        ALU.subtract).then_inc(max_split, 1)
                        dve.wait_ge(max_split, maxi.count(4, 2))
                        V.tensor_copy(max_parts[par][:, 1, :, :], max_rest[par][:, :, :]).then_inc(max_split, 1)
                        dve.wait_ge(max_split, maxi.count(4, 3))
                        V.tensor_tensor(max_parts[par][:, 2, :, :], max_rest[par][:, :, :],
                                        max_parts[par][:, 1, :, :], ALU.subtract).then_inc(max_split, 1)
                    if s == 8 and end.exists:
                        dve.wait_ge(ln2_rstd, end.count(1, 1))
                        norm_apply(xn2[end.parity], x_mid[end.parity], mean_var2[end.parity],
                                   rstd2[end.parity], ln2_dve)
                    if s == 9 and maxi.exists:
                        par = maxi.parity
                        dve.wait_ge(v_ready, maxi.count(1, 1))
                        if maxi.at_least(2):
                            dve.wait_ge(pv_done, maxi.plus(-2).count(NC, NC))
                        V.tensor_copy(k_cur[par][0:KR, :], k_new[par][:, :]).then_inc(kv_moved, 1)
                        V.tensor_copy(v_cur[par][:, :, 0:HD], v_new[par][:, :, :]).then_inc(kv_moved, 1)
                    if s == 11 and end.exists:
                        par = end.parity
                        logits = ps_b[:, 0:NT * NE].rearrange("p (n e) -> p n e", n=NT)
                        dve.wait_ge(logits_done, end.count(1, 1))
                        V.tensor_reduce(top[par][:, :], logits, AX.X, ALU.max).then_inc(route_dve, 1)
                        dve.wait_ge(route_dve, end.count(5, 1))
                        V.tensor_tensor(is_top[par][:, :, :], logits, top[par][:, :].unsqueeze(2).broadcast_to([P, NT, NE]),
                                        ALU.is_equal).then_inc(route_dve, 1)
                        dve.wait_ge(route_dve, end.count(5, 2))
                        V.tensor_tensor(ranked[par][:, :, :], is_top[par][:, :, :],
                                        rank[:, :].unsqueeze(1).broadcast_to([P, NT, NE]), ALU.mult).then_inc(route_dve, 1)
                        dve.wait_ge(route_dve, end.count(5, 3))
                        V.tensor_reduce(top_rank[par][:, :], ranked[par][:, :, :], AX.X, ALU.max
                                        ).then_inc(route_dve, 1)
                        dve.wait_ge(route_dve, end.count(5, 4))
                        V.tensor_tensor(onehot[par][:, :, :], ranked[par][:, :, :],
                                        top_rank[par][:, :].unsqueeze(2).broadcast_to([P, NT, NE]), ALU.is_equal
                                        ).then_inc(route_dve, 1)

            steps(dve, step)

        @block.tensor
        def _(pe):
            MM, TR = nc.tensor.matmul, nc.tensor.transpose
            pe.wait_ge(setup_dve, 3)
            pe.wait_ge(consts_made, 1)
            TR(ps_a[:, 0:NB], c_silu[:, :], ident[0:NB, 0:NB]).then_inc(setup_pe, 1)
            pe.wait_ge(setup_dve, 4)
            for m, part in enumerate((0, 1, 3, 4)):
                MM(ps_a[:, 64 * m:64 * m + NB], wm_sb[:, part * C:(part + 1) * C], c_siluT[:, :],
                   start=True, stop=True)
            MM(ps_b[0:NB, 0:C], c_siluT[:, :], wm_sb[:, 2 * C:3 * C], start=True, stop=True)
            MM(ps_b[0:NB, C:2 * C], c_siluT[:, :], wm_sb[:, 5 * C:6 * C], start=True, stop=True
               ).then_inc(setup_pe, 1)
            pe.wait_ge(setup_ready, 1)

            def scores(b, s):
                c, kind = s // 3, s % 3
                h0, heads = score_chunk(c, kind)
                if s == 0:
                    pe.wait_ge(kv_moved, b.count(2, 2))
                    pe.wait_ge(shift_loaded[b.parity], b.pair_count(48, 48))
                if s >= 3 or b.at_least(1):
                    pe.wait_ge(probs_ready, b.count(CH, s - 2))
                q = q_rows[b.parity][0:KRS, h0:h0 + heads, :]
                key_tile, q = (0, q) if kind < 2 else (1, q[:, :, P:T])
                MM(ps_s[s % 3][:, :], k_cur[b.parity][0:KRS, key_tile * P:(key_tile + 1) * P], q,
                   start=True, stop=False)
                MM(ps_s[s % 3][:, :].rearrange("p (h t) -> p h t", h=heads)[:, :, 0:P], ident_b[:, :],
                   later[:, :].unsqueeze(1).broadcast_to([P, heads, P]), start=False, stop=True
                   ).then_inc(scores_done, 1)

            def max_scores_of(b, m):
                c, kind = m // 3, m % 3
                h0, heads = score_chunk(c, kind)
                if m == 0:
                    pe.wait_ge(qk_dve, b.count(6, 6))
                if kind == 0:
                    pe.wait_ge(q_loaded[b.parity][c], b.pair_count(48, 48))
                if m >= 2 or b.at_least(1):
                    pe.wait_ge(max_taken, b.count(CH, m - 1))
                bk = ps_m[m % 2]
                tile = 1 if kind < 2 else 0
                keys = P * (tile + 1)
                for n in range(heads):
                    MM(bk[:, n * keys:(n + 1) * keys], q_rows[b.parity][0:KR, h0 + n, tile * P:(tile + 1) * P],
                       k_new[b.parity][0:KR, 0:keys], start=(n == 0), stop=False, skip_group_check=True)
                MM(bk[:, :].rearrange("p (h s) -> p h s", h=heads)[:, :, tile * P:keys], ident_b[:, :],
                   future[:, :].unsqueeze(1).broadcast_to([P, heads, P]), start=False, stop=True, skip_group_check=True
                   ).then_inc(max_scores, 1)

            def values(b, c):
                pe.wait_ge(probs_ready, b.count(CH, 3 * c + 3))
                if c == 2:
                    pe.wait_ge(y_copied, b.count(2, 1))
                elif c == 0 and b.at_least(1):
                    pe.wait_ge(y_copied, b.count(2, 0))
                v = v_cur[b.parity]
                at = (c % 2) * T
                for j in range(4):
                    p = probs[(3 * c + j // 2) % 6]
                    MM(ps_y[32 * j:32 * j + VW, at:at + T], v[:, 0, :], p[:, (j % 2) * T:(j % 2 + 1) * T],
                       start=True, stop=False, tile_position=(0, 32 * j))
                p = probs[(3 * c + 2) % 6]
                for j in range(4):
                    last = MM(ps_y[32 * j:32 * j + VW, at + P:at + T], v[:, 1, :], p[:, j * P:(j + 1) * P],
                              start=False, stop=True, tile_position=(0, 32 * j))
                last.then_inc(pv_done, 1)

            def step(i):
                fill, maxi, soft, end, done = i.plus(2), i.plus(1), i, i.plus(-1), i.plus(-2)
                for s in range(CH):
                    if soft.exists:
                        scores(soft, s)
                    if s < NT and done.exists:
                        for half, bk in enumerate((ps_a, ps_b)):
                            if s == 0 and half == 1:
                                pe.wait_ge(route_dve, done.count(5, 5))
                            if s == 0 and half == 0:
                                if soft.exists:
                                    pe.wait_ge(maxT_ready, soft.count(1, 1))
                                else:
                                    pe.wait_ge(expert_taken, done.count(2 * NT, -1))
                            if s > 0:
                                pe.wait_ge(expert_taken, done.count(2 * NT, 2 * (s - 1) + half + 1))
                            MM(bk[:, :], pick3[:, :], be_parts[:, half * W:(half + 1) * W], start=True, stop=False)
                            MM(bk[:, :], h2T[done.parity][:, s * P:(s + 1) * P],
                               we_sb[:, half * W:(half + 1) * W], start=False, stop=True
                               ).then_inc(experts_done, 1)
                    if s == 1 and end.exists:
                        values(end, NC - 1)
                    if s == 2 and fill.exists:
                        pe.wait_ge(ln1_dve, fill.count(7, 7))
                        if done.exists:
                            pe.wait_ge(expert_taken, done.count(2 * NT, 2 * NT - 1))
                        elif soft.exists:
                            pe.wait_ge(maxT_ready, soft.count(1, 1))
                        elif maxi.exists:
                            pe.wait_ge(v_ready, maxi.count(1, 1))
                        for t in range(NT):
                            last = TR(ps_a[:, t * P:(t + 1) * P], xn[fill.parity][:, t, :], ident[:, :])
                        last.then_inc(xnT_done, 1)
                    if s in (3, 5) and end.exists:
                        t = (s - 3) // 2
                        if t == 0:
                            pe.wait_ge(y_copied, end.count(2, 2))
                            if done.exists:
                                pe.wait_ge(expert_taken, done.count(2 * NT, 2 * NT))
                        else:
                            pe.wait_ge(y_normed, end.count(NT, t))
                        for c in range(NC):
                            last = TR(ps_b[:, c * P:(c + 1) * P], y_raw[end.parity][:, c, t * P:(t + 1) * P],
                                      ident[:, :])
                        last.then_inc(y_turned, 1)
                    if s == 4 and fill.exists:
                        pe.wait_ge(hT_ready, fill.count(1, 1))
                        MM(ps_a[0:LAT, 0:T], wd_sb[:, :], hT[fill.parity][:, :], start=True, stop=True
                           ).then_inc(lat_done, 1)
                    if s == 6 and fill.exists:
                        pe.wait_ge(latT_ready, fill.count(1, 1))
                        MM(ps_a[:, 0:T], wq_sb[:, :], latT[fill.parity][:, :], start=True, stop=True)
                        MM(ps_a[0:KR, T:2 * T], wk_rep[:, :], latT[fill.parity][:, :], start=True, stop=True
                           ).then_inc(qk_done, 1)
                    if s == 6 and end.exists:
                        pe.wait_ge(y_normed, end.count(NT, NT))
                        for t in range(NT):
                            last = TR(ps_b[:, t * P:(t + 1) * P], y_tok[end.parity][:, t, :], ident[:, :])
                        last.then_inc(yT_done, 1)
                    if s == 7 and end.exists:
                        pe.wait_ge(yT_ready, end.count(1, 1))
                        for t in range(NT):
                            last = MM(ps_b[:, t * P:(t + 1) * P], yT[end.parity][:, t * P:(t + 1) * P], wp_sb[:, :],
                                      start=True, stop=True)
                        last.then_inc(proj_done, 1)
                    if s == 8 and fill.exists:
                        pe.wait_ge(qk_dve, fill.count(6, 2))
                        for t in range(NT):
                            last = MM(ps_a[:, t * HD:(t + 1) * HD], latT[fill.parity][:, t * P:(t + 1) * P],
                                      wkv_sb[:, HD:2 * HD], start=True, stop=True)
                        last.then_inc(v_done, 1)
                    if s == 9 and end.exists:
                        pe.wait_ge(ln2_dve, end.count(7, 7))
                        for t in range(NT):
                            last = TR(ps_b[:, t * P:(t + 1) * P], xn2[end.parity][:, t, :], ident[:, :])
                        last.then_inc(xn2T_done, 1)
                    if s == 9 and maxi.exists:
                        pe.wait_ge(max_split, maxi.count(4, 4))
                        if fill.exists:
                            pe.wait_ge(v_ready, fill.count(1, 1))
                        TR(ps_a[0:PARTS * NH * NT, 0:P // 2].bitcast(BF16),
                           max_parts[maxi.parity][:, :, :, :].rearrange("p a h n -> p (a h n)"), ident_b[:, :]
                           ).then_inc(maxT_done, 1)
                    if s == 10 and end.exists:
                        pe.wait_ge(h2T_ready, end.count(1, 1))
                        MM(ps_b[0:HID, 0:T], w1_sb[:, :], h2T[end.parity][:, :], start=True, stop=True
                           ).then_inc(hid_done, 1)
                    if s == 11 and end.exists:
                        pe.wait_ge(hidT_ready, end.count(1, 1))
                        for t in range(NT):
                            last = MM(ps_b[:, t * NE:(t + 1) * NE], hidT[end.parity][:, t * P:(t + 1) * P],
                                      w2_sb[:, :], start=True, stop=True)
                        last.then_inc(logits_done, 1)
                    if maxi.exists:
                        for m in range(MAX_FROM[s], MAX_FROM[s] + MAX_CHUNKS[s]):
                            max_scores_of(maxi, m)
                    if s in (4, 7, 10) and soft.exists:
                        values(soft, (s - 4) // 3)

            steps(pe, step)


_NAMES = ["L0_attn_x", "L0_attn_Wc_down", "L0_attn_Wq_up", "L0_attn_Wkv_up", "L0_attn_Wc_proj", "L0_ffn_w1",
          "L0_ffn_b1", "L0_ffn_w2", "L0_ffn_b2", "L0_ffn_expert_W", "L0_ffn_expert_b", "L0_c", "L0_wmod"]


def kernel(**inputs):
    import numpy as np
    from concourse import bacc
    from concourse.bass_utils import run_bass_kernel_spmd

    nc = bacc.Bacc("TRN2", target_bir_lowering=False, num_devices=1)
    arrays, args = {}, []
    for name in _NAMES:
        a = np.ascontiguousarray(inputs[name])
        arrays[f"in_{name}"] = a
        args.append(nc.dram_tensor(f"in_{name}", a.shape, mybir.dt.from_np(a.dtype), kind="ExternalInput").ap())
    nb, t, c = arrays["in_L0_attn_x"].shape
    hd = arrays["in_L0_attn_Wkv_up"].shape[1] // 2
    out = nc.dram_tensor("out_x", (nb, t, c), F32, kind="ExternalOutput").ap()
    q_scratch = nc.dram_tensor("q_scratch", (2, 3 * hd, c // hd, t), BF16, kind="Internal").ap()
    gate_scratch = nc.dram_tensor("gate_scratch", (nb, 2, c), F32, kind="Internal").ap()
    adaln_block(nc, *args, out, q_scratch, gate_scratch)
    r = run_bass_kernel_spmd(nc, [arrays], core_ids=[0])
    return r.results[0]["out_x"]
```

```python
from contextlib import ExitStack

import concourse.bass as bass
from concourse import mybir

F32 = mybir.dt.float32
BF16 = mybir.dt.bfloat16
I32 = mybir.dt.int32
ALU = mybir.AluOpType
ACT = mybir.ActivationFunctionType
AX = mybir.AxisListType


class Batch:

    def __init__(self, pair, ahead, parity, n_batches):
        self.pair, self.ahead, self.parity, self.n_batches = pair, ahead, parity, n_batches

    def plus(self, n):
        whole = self.parity + n
        return Batch(self.pair, self.ahead + whole // 2, whole % 2, self.n_batches)

    @property
    def index(self):
        return self.pair * 2 + (2 * self.ahead + self.parity)

    @property
    def exists(self):
        return not isinstance(self.pair, int) or 0 <= self.index < self.n_batches

    def at_least(self, n):
        return not isinstance(self.pair, int) or self.index >= n

    def count(self, per_batch, k):
        return self.pair * (2 * per_batch) + ((2 * self.ahead + self.parity) * per_batch + k)

    def pair_count(self, per_batch, k):
        return self.pair * per_batch + (self.ahead * per_batch + k)


def adaln_block(nc, x, w_down, w_q, w_kv, w_proj, w1, b1, w2, b2, expert_w, expert_b, cond, w_mod, out,
                q_scratch, gate_scratch):
    NB, T, C = x.shape
    P = 128
    NT = T // P
    LAT = w_down.shape[1]
    HD = w_kv.shape[1] // 2
    NH = C // HD
    NE = expert_w.shape[0]
    HID = w1.shape[1]
    EPS = 1e-5
    SCALE = HD ** -0.5
    NEG = -1e30
    NC = NH // 4
    CH = 3 * NC
    PARTS = 3
    QR = PARTS * HD
    KR = 96
    KRS = KR + PARTS
    W = 512
    VW = 32
    HW = VW // 2
    EB = W // C
    MAX_CHUNKS = [2, 1, 2, 1, 1, 2, 1, 2, 0, 0, 0, 0]
    EXPERT_SLOTS = [3, 6, 8, 10]
    MAXT_SLOT = 9
    EXPERTS_BEFORE = sum(s <= MAXT_SLOT for s in EXPERT_SLOTS)
    LN1_SLOTS = [10, 11]
    SUM_SLOTS = [7, 11]
    MAX_FROM = [sum(MAX_CHUNKS[:s]) for s in range(CH)]

    ctx = ExitStack()
    with ctx:
        def sb(name, shape, dt=F32):
            return ctx.enter_context(nc.sbuf_tensor(name, shape, dt))

        def two(name, shape, dt=F32):
            return [sb(f"{name}{i}", shape, dt) for i in range(2)]

        def sem(name):
            return ctx.enter_context(nc.semaphore(name))

        ident = sb("ident", [P, P])
        ident_b = sb("ident_b", [P, P], BF16)
        future = sb("future", [P, P], BF16)
        later = sb("later", [P, P], BF16)
        minus_half = sb("minus_half", [P, NT])
        rank = sb("rank", [P, NE])
        pick3 = sb("pick3", [P, P], BF16)
        wd_sb = sb("wd_sb", [C, LAT])
        wq_in = sb("wq_in", [P, C])
        wq_sb = sb("wq_sb", [P, NT, C])
        wkv_sb = sb("wkv_sb", [P, 2 * HD])
        wk_rep = sb("wk_rep", [P, NT, KR])
        wv_two = sb("wv_two", [P, NT * HD])
        wp_sb = sb("wp_sb", [C, C])
        w1_sb = sb("w1_sb", [C, HID])
        b1_sb = sb("b1_sb", [P, 1])
        w2_in = sb("w2_in", [P, NE])
        w2_two = sb("w2_two", [P, NT * NE])
        b2_sb = sb("b2_sb", [P, NE])
        we_sb = sb("we_sb", [C, NE * C])
        be_rows = sb("be_rows", [PARTS, NE * C])
        be_hi = sb("be_hi", [PARTS, NE * C], BF16)
        be_rest = sb("be_rest", [PARTS, NE * C])
        be_mid = sb("be_mid", [PARTS, NE * C], BF16)
        be_acc = sb("be_acc", [PARTS, NE * C])
        be_parts = sb("be_parts", [P, NE * C], BF16)
        c_sb = sb("c_sb", [NB, C])
        c_exp = sb("c_exp", [NB, C])
        c_silu = sb("c_silu", [NB, C])
        c_siluT = sb("c_siluT", [C, NB])
        wm_sb = sb("wm_sb", [C, 6 * C])
        mod = sb("mod", [C, 4, NB])
        g_sign = sb("g_sign", [NB, 2, C])
        g_raw = sb("g_raw", [NB, 2, C])
        g_size = sb("g_size", [NB, 2, C])

        x_in = two("x_in", [P, NT, C])
        x_res = two("x_res", [P, NT, C])
        gate_a = two("gate_a", [P, C])
        gate_b = two("gate_b", [P, C])
        stats = two("stats", [P, NT, 6])
        mean_var = two("mean_var", [P, NT, 2])
        var_eps = two("var_eps", [P, NT])
        rstd = two("rstd", [P, NT])
        xn = two("xn", [P, NT, C])
        hT = two("hT", [C, T])
        latT = two("latT", [P, P])
        q_parts = two("q_parts", [C, PARTS, T], BF16)
        q_rest = two("q_rest", [C, T])
        k_rest = two("k_rest", [KR, T])
        k_mid = two("k_mid", [KR, T], BF16)
        k_new = two("k_new", [KR, T], BF16)
        k_cur = two("k_cur", [P, T], BF16)
        v_new = two("v_new", [P, NT, HD])
        v_cur = two("v_cur", [P, 2, NT, VW])
        q_rows = two("q_rows", [P, NH, T], BF16)
        maxes = two("maxes", [P, NH, NT])
        max_rest = two("max_rest", [P, NH, NT])
        max_parts = two("max_parts", [P, PARTS, NH, NT], BF16)
        maxT = two("maxT", [PARTS * NH * NT, P], BF16)
        probs = [sb(f"probs{i}", [P, W]) for i in range(6)]
        y_raw = two("y_raw", [P, NC // 2, T])
        r_den = two("r_den", [P, NT * NH])
        y_tok = two("y_tok", [P, NT, C])
        yT = two("yT", [C, T])
        x_gated = two("x_gated", [P, NT, C])
        x_mid = two("x_mid", [P, NT, C])
        stats2 = two("stats2", [P, NT, 6])
        mean_var2 = two("mean_var2", [P, NT, 2])
        var_eps2 = two("var_eps2", [P, NT])
        rstd2 = two("rstd2", [P, NT])
        xn2 = two("xn2", [P, NT, C])
        h2T = two("h2T", [C, T])
        hidT = two("hidT", [P, P])
        logits = two("logits", [P, NT, NE])
        top = two("top", [P, NT])
        is_top = two("is_top", [P, NT, NE])
        top_rank = two("top_rank", [P, NT])
        ranked = two("ranked", [P, NT, NE])
        onehot = two("onehot", [P, NT, NE])
        chosen = two("chosen", [P, NT, NE, C])
        routed_g = two("routed_g", [P, NT, C])
        x_out = two("x_out", [P, NT, C])

        def bank(name):
            return ctx.enter_context(nc.psum_tensor(name, [P, W], F32))
        ps_s = [bank(f"ps_s{i}") for i in range(3)]
        ps_m = [bank(f"ps_m{i}") for i in range(2)]
        ps_y = bank("ps_y")
        ps_a = bank("ps_a")
        ps_b = bank("ps_b")

        LOADS = 18
        cond_in = sem("cond_in")
        weights_in = sem("weights_in")
        gates_made = sem("gates_made")
        biases_ready = sem("biases_ready")
        consts_made = sem("consts_made")
        gps_step = sem("gps_step")
        setup_act = sem("setup_act")
        setup_dve = sem("setup_dve")
        setup_pe = sem("setup_pe")
        setup_ready = sem("setup_ready")
        gates_out = sem("gates_out")
        x_in_loaded = [sem(f"x_in_loaded{i}") for i in range(2)]
        x_res_loaded = [sem(f"x_res_loaded{i}") for i in range(2)]
        gate_b_loaded = [sem(f"gate_b_loaded{i}") for i in range(2)]
        q_written = [sem(f"q_written{i}") for i in range(2)]
        q_loaded = [[sem(f"q_loaded{i}_{c}") for c in range(NC)] for i in range(2)]
        shift_loaded = [sem(f"shift_loaded{i}") for i in range(2)]
        out_stored = [sem(f"out_stored{i}") for i in range(2)]
        ln1_dve = sem("ln1_dve")
        ln1_rstd = sem("ln1_rstd")
        xnT_done = sem("xnT_done")
        hT_ready = sem("hT_ready")
        lat_done = sem("lat_done")
        latT_ready = sem("latT_ready")
        qk_done = sem("qk_done")
        qk_high = sem("qk_high")
        qk_dve = sem("qk_dve")
        q_low = sem("q_low")
        v_done = sem("v_done")
        v_ready = sem("v_ready")
        max_scores = sem("max_scores")
        max_taken = sem("max_taken")
        max_split = sem("max_split")
        kv_moved = sem("kv_moved")
        maxT_done = sem("maxT_done")
        maxT_ready = sem("maxT_ready")
        scores_done = sem("scores_done")
        probs_ready = sem("probs_ready")
        pv_done = sem("pv_done")
        y_copied = sem("y_copied")
        y_turned = sem("y_turned")
        den_ready = sem("den_ready")
        y_normed = sem("y_normed")
        yT_done = sem("yT_done")
        yT_ready = sem("yT_ready")
        proj_done = sem("proj_done")
        x_mid_dve = sem("x_mid_dve")
        ln2_dve = sem("ln2_dve")
        ln2_rstd = sem("ln2_rstd")
        xn2T_done = sem("xn2T_done")
        h2T_ready = sem("h2T_ready")
        hid_done = sem("hid_done")
        hidT_ready = sem("hidT_ready")
        logits_done = sem("logits_done")
        route_dve = sem("route_dve")
        experts_done = sem("experts_done")
        expert_taken = sem("expert_taken")
        routed_gps = sem("routed_gps")
        out_ready = sem("out_ready")

        sp_went_on = sem("sp_went_on")
        dve_went_on = sem("dve_went_on")

        def steps(engine, step, after_first=lambda: None):
            first_pair, last_pair = 1, (NB - 4) // 2
            for i in range(-3, 2 * first_pair):
                step(Batch(0, i // 2, i % 2, NB))
                if i == -3:
                    after_first()
            with engine.Fori(first_pair, last_pair) as pair:
                step(Batch(pair, 0, 0, NB))
                step(Batch(pair, 0, 1, NB))
            for i in range(2 * last_pair, NB + 2):
                step(Batch(0, i // 2, i % 2, NB))

        def score_chunk(c, kind):
            return (NC * c + 2 * kind, 2) if kind < 2 else (NC * c, 4)

        block = ctx.enter_context(nc.Block())

        @block.sync
        def _(sp):
            def load_x(b):
                src = x[bass.ds(b.index, 1), :, :].rearrange("a (n p) c -> p (a n) c", p=P)
                if b.at_least(2):
                    sp.wait_ge(ln1_dve, b.plus(-2).count(7, 7))
                    sp.sem_inc(sp_went_on, 1)
                sp.dma_start(x_in[b.parity][:, :, :], src).then_inc(x_in_loaded[b.parity], 16)

            two_halves = [(wq_in, w_q), (wkv_sb, w_kv), (w2_in, w2), (b1_sb, b1.rearrange("(m a) -> m a", a=1))]
            loads = [(c_sb[:, :], cond), (wm_sb[:, :], w_mod), (wd_sb[:, :], w_down)]
            loads += [(dst[64 * n:64 * n + 64, :], src) for dst, src in two_halves for n in range(NT)]
            loads += [
                (wp_sb[:, :], w_proj), (w1_sb[:, :], w1),
                (b2_sb[:, :], b2.rearrange("(a e) -> a e", a=1).broadcast_to([P, NE])),
                (we_sb[:, :].rearrange("h (e d) -> h e d", e=NE), expert_w.rearrange("e h d -> h e d")),
            ] + [(be_rows[p:p + 1, :], expert_b.rearrange("(a e) d -> a (e d)", a=1)) for p in range(PARTS)]
            assert LAT == HID == 64 and len(loads) == LOADS
            sp.dma_start(*loads[0]).then_inc(cond_in, 16)
            for dst, src in loads[1:]:
                sp.dma_start(dst, src).then_inc(weights_in, 16)
            load_x(Batch(0, 0, 0, NB))
            load_x(Batch(0, 0, 1, NB))
            def step(i):
                fill, soft, done = i.plus(2), i, i.plus(-2)
                if i.plus(4).exists and i.at_least(-2):
                    load_x(i.plus(4))
                if soft.exists:
                    if soft.at_least(2):
                        sp.wait_ge(x_mid_dve, soft.plus(-2).count(2, 2))
                        sp.sem_inc(sp_went_on, 1)
                    sp.dma_start(x_res[soft.parity][:, :, :],
                                 x[bass.ds(soft.index, 1), :, :].rearrange("a (n p) c -> p (a n) c", p=P)
                                 ).then_inc(x_res_loaded[soft.parity], 16)
                    sp.dma_start(gate_a[soft.parity][:, :],
                                 gate_scratch[bass.ds(soft.index, 1), 0, :].broadcast_to([P, C])
                                 ).then_inc(x_res_loaded[soft.parity], 16)
                if fill.exists:
                    sp.wait_ge(qk_dve, fill.count(6, 6))
                    sp.sem_inc(sp_went_on, 1)
                    sp.wait_ge(q_low, fill.count(1, 1))
                    if fill.at_least(2):
                        for c in range(NC):
                            sp.wait_ge(q_loaded[fill.parity][c], fill.plus(-2).pair_count(48, 48))
                    for pq in range(PARTS):
                        sp.dma_start(
                            q_scratch[fill.parity, pq * HD:(pq + 1) * HD, :, :].rearrange("d h t -> h d t"),
                            q_parts[fill.parity][:, pq, :]).then_inc(q_written[fill.parity], 16)
                    sp.wait_ge(q_written[fill.parity], fill.pair_count(48, 48))
                    sp.sem_inc(sp_went_on, 1)
                    for c in range(NC):
                        if soft.exists:
                            sp.wait_ge(scores_done, soft.count(CH, 3 * c + 3))
                        for pk in range(PARTS):
                            sp.dma_start(q_rows[fill.parity][32 * pk:32 * pk + QR, 4 * c:4 * c + 4, :],
                                         q_scratch[fill.parity, :, 4 * c:4 * c + 4, :]
                                         ).then_inc(q_loaded[fill.parity][c], 16)
                if done.exists:
                    sp.wait_ge(out_ready, done.count(NT, NT))
                    sp.sem_inc(sp_went_on, 1)
                    sp.dma_start(out[bass.ds(done.index, 1), :, :].rearrange("a (n p) c -> p (a n) c", p=P),
                                 x_out[done.parity][:, :, :]).then_inc(out_stored[done.parity], 16)
                if soft.exists:
                    sp.dma_start(gate_b[soft.parity][:, :],
                                 gate_scratch[bass.ds(soft.index, 1), 1, :].broadcast_to([P, C])
                                 ).then_inc(gate_b_loaded[soft.parity], 16)

            sp.wait_ge(gates_made, 1)
            sp.dma_start(gate_scratch, g_size[:, :, :]).then_inc(gates_out, 16)
            sp.wait_ge(gates_out, 16)
            sp.wait_ge(setup_ready, 1)
            steps(sp, step)
            for par in range(2):
                sp.wait_ge(out_stored[par], 16 * NB // 2)

        @block.gpsimd
        def _(gp):
            k = [0]

            def made(ins):
                k[0] += 1
                ins.then_inc(gps_step, 1)
                gp.wait_ge(gps_step, k[0])

            made(gp.memset(ident[:, :], 0.0))
            made(gp.affine_select(out=ident[:, :], in_=ident[:, :], compare_op=ALU.not_equal, fill=1.0, base=0,
                                  pattern=[[-1, P]], channel_multiplier=1))
            gp.tensor_copy(ident_b[:, :], ident[:, :]).then_inc(consts_made, 1)
            made(gp.memset(future[:, :], 0.0))
            made(gp.memset(later[:, :], 0.0))
            made(gp.memset(pick3[:, :], 0.0))
            made(gp.memset(be_parts[:, :], 0.0))
            made(gp.memset(minus_half[:, :], -0.5))
            made(gp.affine_select(out=future[:, :], in_=future[:, :], compare_op=ALU.is_ge, fill=NEG, base=0,
                                  pattern=[[-1, P]], channel_multiplier=1))
            made(gp.affine_select(out=later[:, :], in_=later[:, :], compare_op=ALU.is_ge, fill=NEG, base=0,
                                  pattern=[[1, P]], channel_multiplier=-1))
            gp.memset(pick3[0:PARTS, :], 1.0).then_inc(consts_made, 1)

            def power(dst, src):
                return gp.tensor_tensor(dst, src, minus_half[:, :], ALU.pow)

            def step(i):
                norm, fill, end, done = i.plus(3), i.plus(2), i.plus(-1), i.plus(-2)
                for s in range(CH):
                    if s == 6 and end.exists:
                        gp.wait_ge(ln2_dve, end.count(7, 5))
                        power(rstd2[end.parity][:, :], var_eps2[end.parity][:, :]).then_inc(ln2_rstd, 1)
                    if s == 7 and fill.exists:
                        gp.wait_ge(qk_dve, fill.count(6, 3))
                        gp.tensor_tensor(q_parts[fill.parity][:, 2, :], q_rest[fill.parity][:, :],
                                         q_parts[fill.parity][:, 1, :], ALU.subtract).then_inc(q_low, 1)
                    if s == LN1_SLOTS[0] and norm.exists:
                        gp.wait_ge(ln1_dve, norm.count(7, 5))
                        power(rstd[norm.parity][:, :], var_eps[norm.parity][:, :]).then_inc(ln1_rstd, 1)
                    if s in SUM_SLOTS and done.exists:
                        t = SUM_SLOTS.index(s)
                        gp.wait_ge(expert_taken, done.count(2 * NT, 2 * t + 2))
                        ch = chosen[done.parity]
                        half, k = NE // 2, 0
                        while half:
                            gp.tensor_tensor(ch[:, t, 0:half, :], ch[:, t, 0:half, :], ch[:, t, half:2 * half, :],
                                             ALU.add).then_inc(routed_gps, 1)
                            half, k = half // 2, k + 1
                            gp.wait_ge(routed_gps, done.count(8, 4 * t + k))
                        if t == 0:
                            gp.wait_ge(gate_b_loaded[done.parity], done.pair_count(16, 16))
                        gp.tensor_tensor(routed_g[done.parity][:, t, :], ch[:, t, 0, :],
                                         gate_b[done.parity][:, :], ALU.mult).then_inc(routed_gps, 1)
                        gp.wait_ge(routed_gps, done.count(8, 4 * t + 4))
                        if done.at_least(2):
                            gp.wait_ge(out_stored[done.parity], done.plus(-2).pair_count(16, 16))
                        gp.tensor_tensor(x_out[done.parity][:, t, :], routed_g[done.parity][:, t, :],
                                         x_mid[done.parity][:, t, :], ALU.add).then_inc(out_ready, 1)

            gp.wait_ge(setup_ready, 1)
            steps(gp, step)

        @block.scalar
        def _(act):
            act.wait_ge(cond_in, 16)
            nc.scalar.activation(c_exp[:, :], c_sb[:, :], ACT.Exp, scale=-1.0).then_inc(setup_act, 1)
            act.wait_ge(setup_ready, 1)

            def step(i):
                fill, maxi, soft, end = i.plus(2), i.plus(1), i, i.plus(-1)
                for s in range(CH):
                    if soft.exists:
                        act.wait_ge(scores_done, soft.count(CH, s + 1))
                        if s >= 6 or soft.at_least(1):
                            act.wait_ge(pv_done, soft.count(NC, s // 3 - 1))
                        nc.scalar.activation(probs[s % 6][:, :], ps_s[s % 3][:, :], ACT.Exp,
                                             scale=SCALE).then_inc(probs_ready, 1)
                    if s == 3 and fill.exists:
                        act.wait_ge(xnT_done, fill.count(1, 1))
                        nc.scalar.activation(hT[fill.parity][:, :], ps_b[:, 0:T], ACT.Identity,
                                             bias=mod[:, 0, bass.ds(fill.index, 1)],
                                             scale=mod[:, 1, bass.ds(fill.index, 1)]).then_inc(hT_ready, 1)
                    if s == 1 and end.exists:
                        act.wait_ge(pv_done, end.count(NC, NC))
                        nc.scalar.activation(y_raw[end.parity][:, :, :],
                                             ps_y[:, :].rearrange("p (c t) -> p c t", c=2), ACT.Copy
                                             ).then_inc(y_copied, 1)
                    if s == 6 and fill.exists:
                        act.wait_ge(lat_done, fill.count(1, 1))
                        nc.scalar.activation(latT[fill.parity][:, :], ps_b[:, 0:P], ACT.Copy
                                             ).then_inc(latT_ready, 1)
                    if s == 7 and fill.exists:
                        act.wait_ge(qk_done, fill.count(1, 1))
                        if fill.at_least(2):
                            act.wait_ge(q_written[fill.parity], fill.plus(-2).pair_count(48, 48))
                        nc.scalar.activation(q_parts[fill.parity][:, 0, :], ps_b[:, 0:T], ACT.Copy
                                             ).then_inc(qk_high, 1)
                        nc.scalar.activation(k_new[fill.parity][:, :], ps_b[0:KR, T:2 * T], ACT.Copy
                                             ).then_inc(qk_high, 1)
                    if s == 4 and end.exists:
                        act.wait_ge(yT_done, end.count(1, 1))
                        nc.scalar.activation(yT[end.parity][:, :], ps_b[:, 0:T], ACT.Copy).then_inc(yT_ready, 1)
                    if s == 8 and fill.exists:
                        act.wait_ge(v_done, fill.count(1, 1))
                        nc.scalar.activation(v_new[fill.parity][:, :, :],
                                             ps_b[:, 0:NT * HD].rearrange("p (n d) -> p n d", n=NT), ACT.Copy
                                             ).then_inc(v_ready, 1)
                    if s == MAXT_SLOT and maxi.exists:
                        act.wait_ge(maxT_done, maxi.count(1, 1))
                        nc.scalar.activation(maxT[maxi.parity][:, :],
                                             ps_a[0:PARTS * NH * NT, 0:P // 2].bitcast(BF16), ACT.Copy
                                             ).then_inc(maxT_ready, 1)
                    if s == 9 and end.exists:
                        act.wait_ge(xn2T_done, end.count(1, 1))
                        nc.scalar.activation(h2T[end.parity][:, :], ps_b[:, 0:T], ACT.Identity,
                                             bias=mod[:, 2, bass.ds(end.index, 1)],
                                             scale=mod[:, 3, bass.ds(end.index, 1)]).then_inc(h2T_ready, 1)
                    if s == MAXT_SLOT and maxi.exists:
                        act.wait_ge(maxT_ready, maxi.count(1, 1))
                        act.dma_start(q_rows[maxi.parity][KR:KR + PARTS, :, :], maxT[maxi.parity][:, :]
                                      ).then_inc(shift_loaded[maxi.parity], 16)
                    if s == 11 and end.exists:
                        act.wait_ge(hid_done, end.count(1, 1))
                        nc.scalar.activation(hidT[end.parity][:, :], ps_b[:, 0:P], ACT.Relu,
                                             bias=b1_sb[:, :]).then_inc(hidT_ready, 1)

            steps(act, step)

        @block.vector
        def _(dve):
            n = [0]

            def then(ins):
                n[0] += 1
                ins.then_inc(setup_dve, 1)
                dve.wait_ge(setup_dve, n[0])

            V = nc.vector
            for e in range(NE):
                V.memset(rank[:, e:e + 1], float(NE - e))
            for par in range(2):
                V.memset(v_cur[par][:, :, :, :], 0.0)
                V.memset(k_cur[par][KR:KR + 32, :], -1.0)
            V.memset(wq_sb[:, :, :], 0.0)
            V.memset(wk_rep[:, :, :], 0.0)
            V.memset(wv_two[:, :], 0.0)
            V.memset(w2_two[:, :], 0.0)
            for par in range(2):
                then(V.memset(q_rows[par][:, :, :], 0.0))
            for par in range(2):
                for u in range(2):
                    V.memset(v_cur[par][:, u, :, HW * u + HD:HW * u + HD + 1], 1.0)
            dve.wait_ge(setup_act, 1)
            then(V.tensor_scalar(c_exp[:, :], c_exp[:, :], 1.0, None, ALU.add))
            then(V.reciprocal(c_exp[:, :], c_exp[:, :]))
            then(V.tensor_tensor(c_silu[:, :], c_sb[:, :], c_exp[:, :], ALU.mult))
            dve.wait_ge(setup_pe, 1)
            then(V.tensor_copy(c_siluT[:, :], ps_a[:, 0:NB]))
            dve.wait_ge(setup_pe, 2)
            gv = ps_b[0:NB, 0:2 * C].rearrange("b (g c) -> b g c", g=2)
            then(V.tensor_scalar(g_sign[:, :, :], gv, 0.0, 2.0, ALU.is_ge, ALU.mult))
            then(V.tensor_copy(g_raw[:, :, :], gv))
            for m in range(4):
                then(V.tensor_scalar(mod[:, m, :], ps_a[:, 64 * m:64 * m + NB], float(m % 2), None, ALU.add))
            then(V.scalar_tensor_tensor(g_size[:, :, :], g_raw[:, :, :], -1.0, g_raw[:, :, :], ALU.mult, ALU.max))
            then(V.tensor_scalar(g_size[:, :, :], g_size[:, :, :], 0.25, None, ALU.max))
            V.scalar_tensor_tensor(g_size[:, :, :], g_sign[:, :, :], -1.0, g_size[:, :, :],
                                   ALU.add, ALU.mult).then_inc(gates_made, 1)
            dve.wait_ge(weights_in, 16 * (LOADS - 1))
            for t in range(NT):
                half = slice(64 * t, 64 * t + 64)
                for r in range(2):
                    then(V.tensor_copy(
                        wq_sb[half, t, r * 64:r * 64 + 64].rearrange("l (u j d) -> l u j d", u=2, j=4),
                        wq_in[half, r * 64:r * 64 + 64].rearrange("l (j u d) -> l u j d", u=2, j=4)))
                for pk in range(PARTS):
                    then(V.tensor_copy(wk_rep[half, t, 32 * pk:32 * pk + QR].rearrange("l (a d) -> l a d", a=PARTS),
                                       wkv_sb[half, 0:HD].unsqueeze(1).broadcast_to([64, PARTS, HD])))
                then(V.tensor_copy(wv_two[half, t * HD:(t + 1) * HD], wkv_sb[half, HD:2 * HD]))
                then(V.tensor_copy(w2_two[half, t * NE:(t + 1) * NE], w2_in[half, :]))
            dve.wait_ge(consts_made, 2)
            V.memset(top[0][:, :], 0.0).then_inc(setup_ready, 1)

            def split_biases():
                then(V.tensor_copy(be_hi[:, :], be_rows[:, :]))
                then(V.tensor_tensor(be_rest[:, :], be_rows[:, :], be_hi[:, :], ALU.subtract))
                then(V.tensor_copy(be_mid[:, :], be_rest[:, :]))
                then(V.tensor_tensor(be_rest[:, :], be_rest[:, :], be_mid[:, :], ALU.subtract))
                then(V.tensor_scalar(be_acc[:, :], be_hi[:, :], ident[0:PARTS, 0:1], None, ALU.mult))
                then(V.scalar_tensor_tensor(be_acc[:, :], be_mid[:, :], ident[0:PARTS, 1:2], be_acc[:, :],
                                            ALU.mult, ALU.add))
                V.scalar_tensor_tensor(be_parts[0:PARTS, :], be_rest[:, :], ident[0:PARTS, 2:3], be_acc[:, :],
                                       ALU.mult, ALU.add).then_inc(biases_ready, 1)

            def norm_stats(src, st, mv, ve, done, b):
                for t in range(NT):
                    V.bn_stats(st[:, t, :], src[:, t, :]).then_inc(done, 1)
                dve.wait_ge(done, b.count(7, 2))
                dve.sem_inc(dve_went_on, 1)
                for t in range(NT):
                    V.bn_aggr(mv[:, t, :], st[:, t, :]).then_inc(done, 1)
                dve.wait_ge(done, b.count(7, 4))
                V.tensor_scalar(ve[:, :], mv[:, :, 1], EPS, None, ALU.add).then_inc(done, 1)

            def norm_apply(dst, src, mv, rs, done):
                for t in range(NT):
                    V.tensor_scalar(dst[:, t, :], src[:, t, :], mv[:, t, 0:1], rs[:, t:t + 1],
                                    ALU.subtract, ALU.mult).then_inc(done, 1)

            def take_max(b, m):
                c, kind = m // 3, m % 3
                h0, heads = score_chunk(c, kind)
                dve.wait_ge(max_scores, b.count(CH, m + 1))
                V.tensor_reduce(maxes[b.parity][:, h0:h0 + heads, 1 if kind < 2 else 0],
                                ps_m[m % 2][:, :].rearrange("p (h s) -> p h s", h=heads),
                                AX.X, ALU.max).then_inc(max_taken, 1)

            def take_expert(b, n):
                t, half = n // 2, n % 2
                dve.wait_ge(experts_done, b.count(2 * NT, n + 1))
                if n == 0:
                    dve.wait_ge(route_dve, b.count(6, 6))
                V.tensor_tensor(chosen[b.parity][:, t, half * EB:(half + 1) * EB, :],
                                ps_a[:, :].rearrange("p (e c) -> p e c", e=EB),
                                onehot[b.parity][:, t, half * EB:(half + 1) * EB].unsqueeze(2).broadcast_to(
                                    [P, EB, C]), ALU.mult).then_inc(expert_taken, 1)

            def step(i):
                norm, fill, maxi, soft, end, done = i.plus(3), i.plus(2), i.plus(1), i, i.plus(-1), i.plus(-2)
                for s in range(CH):
                    if s == 0 and done.exists:
                        par = done.parity
                        dve.wait_ge(logits_done, done.count(1, 1))
                        V.tensor_tensor(logits[par][:, :, :],
                                        ps_b[:, 0:NT * NE].rearrange("p (n e) -> p n e", n=NT),
                                        b2_sb[:, :].unsqueeze(1).broadcast_to([P, NT, NE]), ALU.add
                                        ).then_inc(route_dve, 1)
                        dve.wait_ge(route_dve, done.count(6, 1))
                        V.tensor_reduce(top[par][:, :], logits[par][:, :, :], AX.X, ALU.max
                                        ).then_inc(route_dve, 1)
                        dve.wait_ge(route_dve, done.count(6, 2))
                        V.tensor_tensor(is_top[par][:, :, :], logits[par][:, :, :],
                                        top[par][:, :].unsqueeze(2).broadcast_to([P, NT, NE]),
                                        ALU.is_equal).then_inc(route_dve, 1)
                        dve.wait_ge(route_dve, done.count(6, 3))
                        V.tensor_tensor(ranked[par][:, :, :], is_top[par][:, :, :],
                                        rank[:, :].unsqueeze(1).broadcast_to([P, NT, NE]), ALU.mult
                                        ).then_inc(route_dve, 1)
                        dve.wait_ge(route_dve, done.count(6, 4))
                        V.tensor_reduce(top_rank[par][:, :], ranked[par][:, :, :], AX.X, ALU.max
                                        ).then_inc(route_dve, 1)
                        dve.wait_ge(route_dve, done.count(6, 5))
                        V.tensor_tensor(onehot[par][:, :, :], ranked[par][:, :, :],
                                        top_rank[par][:, :].unsqueeze(2).broadcast_to([P, NT, NE]), ALU.is_equal
                                        ).then_inc(route_dve, 1)
                    if s == 2 and end.exists:
                        dve.wait_ge(y_turned, end.count(1, 1))
                        turned = ps_b[:, :].rearrange("p (h w) -> p h w", w=HW)
                        V.reciprocal(r_den[end.parity][:, :], turned[:, :, HD]).then_inc(den_ready, 1)
                        dve.wait_ge(den_ready, end.count(1, 1))
                        V.tensor_tensor(y_tok[end.parity][:, :, :].rearrange("p n (h d) -> p (n h) d", d=HD),
                                        turned[:, :, 0:HD],
                                        r_den[end.parity][:, :].unsqueeze(2).broadcast_to([P, NT * NH, HD]),
                                        ALU.mult).then_inc(y_normed, 1)
                    if s == 7 and fill.exists:
                        par = fill.parity
                        dve.wait_ge(qk_high, fill.count(2, 2))
                        V.tensor_tensor(q_rest[par][:, :], ps_b[:, 0:T], q_parts[par][:, 0, :],
                                        ALU.subtract).then_inc(qk_dve, 1)
                        V.tensor_tensor(k_rest[par][:, :], ps_b[0:KR, T:2 * T], k_new[par][:, :],
                                        ALU.subtract).then_inc(qk_dve, 1)
                        dve.wait_ge(qk_dve, fill.count(6, 2))
                        V.tensor_copy(q_parts[par][:, 1, :], q_rest[par][:, :]).then_inc(qk_dve, 1)
                        V.tensor_copy(k_mid[par][64:96, :], k_rest[par][64:96, :]).then_inc(qk_dve, 1)
                        V.tensor_copy(k_new[par][32:64, :], k_rest[par][32:64, :]).then_inc(qk_dve, 1)
                        dve.wait_ge(qk_dve, fill.count(6, 4))
                        V.tensor_tensor(k_new[par][64:96, :], k_rest[par][64:96, :], k_mid[par][64:96, :],
                                        ALU.subtract).then_inc(qk_dve, 1)
                    if s == 5 and end.exists:
                        par = end.parity
                        dve.wait_ge(proj_done, end.count(1, 1))
                        dve.wait_ge(x_res_loaded[par], end.pair_count(32, 32))
                        V.tensor_tensor(x_gated[par][:, :, :], ps_b[:, 0:T].rearrange("p (n c) -> p n c", n=NT),
                                        gate_a[par][:, :].unsqueeze(1).broadcast_to([P, NT, C]), ALU.mult
                                        ).then_inc(x_mid_dve, 1)
                        dve.wait_ge(x_mid_dve, end.count(2, 1))
                        if end.at_least(2):
                            dve.wait_ge(out_ready, end.plus(-2).count(NT, NT))
                        V.tensor_tensor(x_mid[par][:, :, :], x_gated[par][:, :, :], x_res[par][:, :, :],
                                        ALU.add).then_inc(x_mid_dve, 1)
                        dve.wait_ge(x_mid_dve, end.count(2, 2))
                        norm_stats(x_mid[par], stats2[par], mean_var2[par], var_eps2[par], ln2_dve, end)
                    if s == 8 and maxi.exists:
                        par = maxi.parity
                        dve.wait_ge(max_taken, maxi.count(CH, CH))
                        V.tensor_copy(max_parts[par][:, 0, :, :], maxes[par][:, :, :]).then_inc(max_split, 1)
                        dve.wait_ge(max_split, maxi.count(4, 1))
                        V.tensor_tensor(max_rest[par][:, :, :], maxes[par][:, :, :], max_parts[par][:, 0, :, :],
                                        ALU.subtract).then_inc(max_split, 1)
                        dve.wait_ge(max_split, maxi.count(4, 2))
                        V.tensor_copy(max_parts[par][:, 1, :, :], max_rest[par][:, :, :]).then_inc(max_split, 1)
                        dve.wait_ge(max_split, maxi.count(4, 3))
                        V.tensor_tensor(max_parts[par][:, 2, :, :], max_rest[par][:, :, :],
                                        max_parts[par][:, 1, :, :], ALU.subtract).then_inc(max_split, 1)
                    if s == 7 and end.exists:
                        dve.wait_ge(ln2_rstd, end.count(1, 1))
                        norm_apply(xn2[end.parity], x_mid[end.parity], mean_var2[end.parity],
                                   rstd2[end.parity], ln2_dve)
                    if s == 9 and maxi.exists:
                        par = maxi.parity
                        dve.wait_ge(v_ready, maxi.count(1, 1))
                        if maxi.at_least(2):
                            dve.wait_ge(pv_done, maxi.plus(-2).count(NC, NC))
                        V.tensor_copy(k_cur[par][0:KR, :], k_new[par][:, :]).then_inc(kv_moved, 1)
                        for u in range(2):
                            V.tensor_copy(v_cur[par][:, u, :, HW * u:HW * u + HD], v_new[par][:, :, :]
                                          ).then_inc(kv_moved, 1)
                    if s == LN1_SLOTS[0] and norm.exists:
                        dve.wait_ge(x_in_loaded[norm.parity], norm.pair_count(16, 16))
                        norm_stats(x_in[norm.parity], stats[norm.parity], mean_var[norm.parity],
                                   var_eps[norm.parity], ln1_dve, norm)
                    if s == LN1_SLOTS[1] and norm.exists:
                        dve.wait_ge(ln1_rstd, norm.count(1, 1))
                        norm_apply(xn[norm.parity], x_in[norm.parity], mean_var[norm.parity],
                                   rstd[norm.parity], ln1_dve)
                    if s in EXPERT_SLOTS and done.exists:
                        take_expert(done, EXPERT_SLOTS.index(s))
                    if maxi.exists:
                        for m in range(MAX_FROM[s], MAX_FROM[s] + MAX_CHUNKS[s]):
                            take_max(maxi, m)

            steps(dve, step, split_biases)

        @block.tensor
        def _(pe):
            MM, TR = nc.tensor.matmul, nc.tensor.transpose
            pe.wait_ge(setup_dve, 5)
            pe.wait_ge(consts_made, 1)
            pe.wait_ge(weights_in, 16 * (LOADS - 1))
            TR(ps_a[:, 0:NB], c_silu[:, :], ident[0:NB, 0:NB]).then_inc(setup_pe, 1)
            pe.wait_ge(setup_dve, 6)
            for m, part in enumerate((0, 1, 3, 4)):
                MM(ps_a[:, 64 * m:64 * m + NB], wm_sb[:, part * C:(part + 1) * C], c_siluT[:, :],
                   start=True, stop=True)
            MM(ps_b[0:NB, 0:C], c_siluT[:, :], wm_sb[:, 2 * C:3 * C], start=True, stop=True)
            MM(ps_b[0:NB, C:2 * C], c_siluT[:, :], wm_sb[:, 5 * C:6 * C], start=True, stop=True
               ).then_inc(setup_pe, 1)
            pe.wait_ge(setup_ready, 1)

            def scores(b, s):
                c, kind = s // 3, s % 3
                h0, heads = score_chunk(c, kind)
                if s == 0:
                    pe.wait_ge(kv_moved, b.count(3, 3))
                    pe.wait_ge(shift_loaded[b.parity], b.pair_count(16, 16))
                if s >= 3 or b.at_least(1):
                    pe.wait_ge(probs_ready, b.count(CH, s - 2))
                q = q_rows[b.parity][0:KRS, h0:h0 + heads, :]
                key_tile, q = (0, q) if kind < 2 else (1, q[:, :, P:T])
                MM(ps_s[s % 3][:, :], k_cur[b.parity][0:KRS, key_tile * P:(key_tile + 1) * P], q,
                   start=True, stop=False)
                MM(ps_s[s % 3][:, :].rearrange("p (h t) -> p h t", h=heads)[:, :, 0:P], ident_b[:, :],
                   later[:, :].unsqueeze(1).broadcast_to([P, heads, P]), start=False, stop=True
                   ).then_inc(scores_done, 1)

            def max_scores_of(b, m):
                c, kind = m // 3, m % 3
                h0, heads = score_chunk(c, kind)
                if m == 0:
                    pe.wait_ge(qk_dve, b.count(6, 6))
                if kind == 0:
                    pe.wait_ge(q_loaded[b.parity][c], b.pair_count(48, 48))
                if m >= 2 or b.at_least(1):
                    pe.wait_ge(max_taken, b.count(CH, m - 1))
                bk = ps_m[m % 2]
                tile = 1 if kind < 2 else 0
                keys = P * (tile + 1)
                for n in range(heads):
                    MM(bk[:, n * keys:(n + 1) * keys], q_rows[b.parity][0:KR, h0 + n, tile * P:(tile + 1) * P],
                       k_new[b.parity][0:KR, 0:keys], start=(n == 0), stop=False, skip_group_check=True)
                MM(bk[:, :].rearrange("p (h s) -> p h s", h=heads)[:, :, tile * P:keys], ident_b[:, :],
                   future[:, :].unsqueeze(1).broadcast_to([P, heads, P]), start=False, stop=True, skip_group_check=True
                   ).then_inc(max_scores, 1)

            def values(b, c):
                pe.wait_ge(probs_ready, b.count(CH, 3 * c + 3))
                if c == 0 and b.at_least(1):
                    pe.wait_ge(y_copied, b.count(1, 0))
                r, u = c // 2, c % 2
                v = v_cur[b.parity]
                at = r * T
                for j in range(4):
                    p = probs[(3 * c + j // 2) % 6]
                    MM(ps_y[32 * j:32 * j + VW, at:at + T], v[:, u, 0, :], p[:, (j % 2) * T:(j % 2 + 1) * T],
                       start=(u == 0), stop=False, tile_position=(0, 32 * j))
                p = probs[(3 * c + 2) % 6]
                for j in range(4):
                    last = MM(ps_y[32 * j:32 * j + VW, at + P:at + T], v[:, u, 1, :], p[:, j * P:(j + 1) * P],
                              start=False, stop=(u == 1), tile_position=(0, 32 * j))
                last.then_inc(pv_done, 1)

            def step(i):
                fill, maxi, soft, end, done = i.plus(2), i.plus(1), i, i.plus(-1), i.plus(-2)
                for s in range(CH):
                    if soft.exists:
                        scores(soft, s)
                    if s == 1 and end.exists:
                        values(end, NC - 1)
                    if s == 0 and done.exists:
                        pe.wait_ge(hidT_ready, done.count(1, 1))
                        MM(ps_b[:, 0:NT * NE], hidT[done.parity][:, :], w2_two[:, :], start=True, stop=True
                           ).then_inc(logits_done, 1)
                    if s == 2 and end.exists:
                        pe.wait_ge(y_copied, end.count(1, 1))
                        if done.exists:
                            pe.wait_ge(route_dve, done.count(6, 1))
                        elif soft.exists:
                            pe.wait_ge(v_ready, maxi.count(1, 1))
                        for t in range(NT):
                            for r in range(NC // 2):
                                last = TR(ps_b[:, (2 * t + r) * P:(2 * t + r + 1) * P],
                                          y_raw[end.parity][:, r, t * P:(t + 1) * P], ident[:, :])
                        last.then_inc(y_turned, 1)
                    if s == 3 and fill.exists:
                        pe.wait_ge(ln1_dve, fill.count(7, 7))
                        if end.exists:
                            pe.wait_ge(y_normed, end.count(1, 1))
                        elif fill.at_least(1):
                            pe.wait_ge(v_ready, fill.count(1, 0))
                        for t in range(NT):
                            last = TR(ps_b[:, t * P:(t + 1) * P], xn[fill.parity][:, t, :], ident[:, :])
                        last.then_inc(xnT_done, 1)
                    if s == 4 and end.exists:
                        if fill.exists:
                            pe.wait_ge(hT_ready, fill.count(1, 1))
                        pe.wait_ge(y_normed, end.count(1, 1))
                        for t in range(NT):
                            last = TR(ps_b[:, t * P:(t + 1) * P], y_tok[end.parity][:, t, :], ident[:, :])
                        last.then_inc(yT_done, 1)
                    if s == 5 and end.exists:
                        pe.wait_ge(yT_ready, end.count(1, 1))
                        for t in range(NT):
                            last = MM(ps_b[:, t * P:(t + 1) * P], yT[end.parity][:, t * P:(t + 1) * P], wp_sb[:, :],
                                      start=True, stop=True)
                        last.then_inc(proj_done, 1)
                    if s == 6 and fill.exists:
                        pe.wait_ge(hT_ready, fill.count(1, 1))
                        if end.exists:
                            pe.wait_ge(x_mid_dve, end.count(2, 1))
                        for t in range(NT):
                            last = MM(ps_b[LAT * t:LAT * (t + 1), 0:P], wd_sb[:, :],
                                      hT[fill.parity][:, t * P:(t + 1) * P], start=True, stop=True,
                                      tile_position=(0, LAT * t))
                        last.then_inc(lat_done, 1)
                    if s == 7 and fill.exists:
                        pe.wait_ge(latT_ready, fill.count(1, 1))
                        for at, rows, w in ((0, C, wq_sb), (T, KR, wk_rep)):
                            for t in range(NT):
                                last = MM(ps_b[0:rows, at + t * P:at + (t + 1) * P], w[:, t, :],
                                          latT[fill.parity][:, :], start=True, stop=True)
                        last.then_inc(qk_done, 1)
                    if s == 8 and fill.exists:
                        pe.wait_ge(qk_dve, fill.count(6, 2))
                        MM(ps_b[:, 0:NT * HD], latT[fill.parity][:, :], wv_two[:, :], start=True, stop=True
                           ).then_inc(v_done, 1)
                    if s == 9 and end.exists:
                        pe.wait_ge(ln2_dve, end.count(7, 7))
                        if fill.exists:
                            pe.wait_ge(v_ready, fill.count(1, 1))
                        for t in range(NT):
                            last = TR(ps_b[:, t * P:(t + 1) * P], xn2[end.parity][:, t, :], ident[:, :])
                        last.then_inc(xn2T_done, 1)
                    if s == 11 and end.exists:
                        pe.wait_ge(h2T_ready, end.count(1, 1))
                        for t in range(NT):
                            last = MM(ps_b[HID * t:HID * (t + 1), 0:P], w1_sb[:, :],
                                      h2T[end.parity][:, t * P:(t + 1) * P], start=True, stop=True,
                                      tile_position=(0, HID * t))
                        last.then_inc(hid_done, 1)
                    if s in EXPERT_SLOTS and done.exists:
                        n = EXPERT_SLOTS.index(s)
                        t, half = n // 2, n % 2
                        if n == EXPERTS_BEFORE and maxi.exists:
                            pe.wait_ge(maxT_ready, maxi.count(1, 1))
                        elif n > 0 or done.at_least(1):
                            pe.wait_ge(expert_taken, done.count(2 * NT, n))
                        elif soft.exists:
                            pe.wait_ge(maxT_ready, soft.count(1, 1))
                        if n == 0 and isinstance(done.pair, int):
                            pe.wait_ge(biases_ready, 1)
                        MM(ps_a[:, :], pick3[:, :], be_parts[:, half * W:(half + 1) * W], start=True, stop=False)
                        MM(ps_a[:, :], h2T[done.parity][:, t * P:(t + 1) * P],
                           we_sb[:, half * W:(half + 1) * W], start=False, stop=True
                           ).then_inc(experts_done, 1)
                    if s == MAXT_SLOT and maxi.exists:
                        pe.wait_ge(max_split, maxi.count(4, 4))
                        if done.exists:
                            pe.wait_ge(expert_taken, done.count(2 * NT, EXPERTS_BEFORE))
                        TR(ps_a[0:PARTS * NH * NT, 0:P // 2].bitcast(BF16),
                           max_parts[maxi.parity][:, :, :, :].rearrange("p a h n -> p (a h n)"), ident_b[:, :]
                           ).then_inc(maxT_done, 1)
                    if maxi.exists:
                        for m in range(MAX_FROM[s], MAX_FROM[s] + MAX_CHUNKS[s]):
                            max_scores_of(maxi, m)
                    if s in (4, 7, 10) and soft.exists:
                        values(soft, (s - 4) // 3)

            steps(pe, step)


_NAMES = ["L0_attn_x", "L0_attn_Wc_down", "L0_attn_Wq_up", "L0_attn_Wkv_up", "L0_attn_Wc_proj", "L0_ffn_w1",
          "L0_ffn_b1", "L0_ffn_w2", "L0_ffn_b2", "L0_ffn_expert_W", "L0_ffn_expert_b", "L0_c", "L0_wmod"]


def kernel(**inputs):
    import numpy as np
    from concourse import bacc
    from concourse.bass_utils import run_bass_kernel_spmd

    nc = bacc.Bacc("TRN2", target_bir_lowering=False, num_devices=1)
    arrays, args = {}, []
    for name in _NAMES:
        a = np.ascontiguousarray(inputs[name])
        arrays[f"in_{name}"] = a
        args.append(nc.dram_tensor(f"in_{name}", a.shape, mybir.dt.from_np(a.dtype), kind="ExternalInput").ap())
    nb, t, c = arrays["in_L0_attn_x"].shape
    hd = arrays["in_L0_attn_Wkv_up"].shape[1] // 2
    out = nc.dram_tensor("out_x", (nb, t, c), F32, kind="ExternalOutput").ap()
    q_scratch = nc.dram_tensor("q_scratch", (2, 3 * hd, c // hd, t), BF16, kind="Internal").ap()
    gate_scratch = nc.dram_tensor("gate_scratch", (nb, 2, c), F32, kind="Internal").ap()
    adaln_block(nc, *args, out, q_scratch, gate_scratch)
    r = run_bass_kernel_spmd(nc, [arrays], core_ids=[0])
    return r.results[0]["out_x"]
```

```python
from contextlib import ExitStack

import concourse.bass as bass
from concourse import mybir

F32 = mybir.dt.float32
BF16 = mybir.dt.bfloat16
ALU = mybir.AluOpType
ACT = mybir.ActivationFunctionType
AX = mybir.AxisListType


class Batch:

    def __init__(self, pair, ahead, parity, n_batches):
        self.pair, self.ahead, self.parity, self.n_batches = pair, ahead, parity, n_batches

    def plus(self, n):
        whole = self.parity + n
        return Batch(self.pair, self.ahead + whole // 2, whole % 2, self.n_batches)

    @property
    def index(self):
        return self.pair * 2 + (2 * self.ahead + self.parity)

    @property
    def exists(self):
        return not isinstance(self.pair, int) or 0 <= self.index < self.n_batches

    def at_least(self, n):
        return not isinstance(self.pair, int) or self.index >= n

    def count(self, per_batch, k):
        return self.pair * (2 * per_batch) + ((2 * self.ahead + self.parity) * per_batch + k)

    def pair_count(self, per_batch, k):
        return self.pair * per_batch + (self.ahead * per_batch + k)


def adaln_block(nc, x, w_down, w_q, w_kv, w_proj, w1, b1, w2, b2, expert_w, expert_b, cond, w_mod, out,
                q_scratch, gate_scratch):
    NB, T, C = x.shape
    P = 128
    NT = T // P
    LAT = w_down.shape[1]
    HD = w_kv.shape[1] // 2
    NH = C // HD
    NE = expert_w.shape[0]
    HID = w1.shape[1]
    EPS = 1e-5
    SCALE = HD ** -0.5
    NEG = -1e30
    NC = NH // 4
    CH = 3 * NC
    PARTS = 3
    QR = PARTS * HD
    KR = 96
    PIECE = 64
    PIECES = T // PIECE
    MR = KR + PIECES
    KRS = MR + PARTS
    W = 512
    VW = 32
    HW = VW // 2
    BR = 32 * (PARTS - 1) + 1
    EB = W // C
    AT = dict(
        logits=0, last_values=0, turn_y=2, turn_x=3, turn_y_back=4, project=5, latent=5,
        qk=6, v=9, turn_mid=10, hidden=11, turn_max=9, experts=[2, 7, 9, 10], middle_qk=6,
        route=0, normalise_y=2, middle=5, split_qk=7, norm_mid=8,
        split_max=8, move_kv=7, stats_x=8, norm_x=9, take_experts=[4, 7, 9, 10],
        rstd_mid=3, low_q=5, rstd_x=10, sum_experts=[7, 10])
    MAX_CHUNKS = [1, 1, 2, 2, 2, 2, 0, 2, 0, 0, 0, 0]
    EXPERTS_BEFORE = sum(s <= AT["turn_max"] for s in AT["experts"])
    MAXT_BANK = EXPERTS_BEFORE % 2
    MAX_FROM = [sum(MAX_CHUNKS[:s]) for s in range(CH)]

    ctx = ExitStack()
    with ctx:
        def sb(name, shape, dt=F32):
            return ctx.enter_context(nc.sbuf_tensor(name, shape, dt))

        def two(name, shape, dt=F32):
            return [sb(f"{name}{i}", shape, dt) for i in range(2)]

        def sem(name):
            return ctx.enter_context(nc.semaphore(name))

        ident = sb("ident", [P, P])
        ident_b = sb("ident_b", [P, P], BF16)
        future = sb("future", [P, P], BF16)
        later = sb("later", [P, P], BF16)
        key_block = sb("key_block", [PIECES, T], BF16)
        before_block = sb("before_block", [PIECES, T], BF16)
        minus_half = sb("minus_half", [P, NT])
        rank = sb("rank", [P, NE])
        pick3 = sb("pick3", [P, P], BF16)
        wd_sb = sb("wd_sb", [C, LAT])
        wq_in = sb("wq_in", [P, C])
        wq_sb = sb("wq_sb", [P, NT, C])
        wkv_sb = sb("wkv_sb", [P, 2 * HD])
        wk_rep = sb("wk_rep", [P, NT, KR])
        wv_two = sb("wv_two", [P, NT * HD])
        wp_sb = sb("wp_sb", [C, C])
        w1_sb = sb("w1_sb", [C, HID])
        b1_sb = sb("b1_sb", [P, 1])
        w2_in = sb("w2_in", [P, NE])
        w2_two = sb("w2_two", [P, NT * NE])
        b2_sb = sb("b2_sb", [P, NE])
        we_sb = sb("we_sb", [C, NE * C])
        be_rows = sb("be_rows", [BR, NE * C])
        be_hi = sb("be_hi", [BR, NE * C], BF16)
        be_rest = sb("be_rest", [BR, NE * C])
        be_mid = sb("be_mid", [BR, NE * C], BF16)
        be_parts = sb("be_parts", [P, NE * C], BF16)
        c_sb = sb("c_sb", [NB, C])
        c_exp = sb("c_exp", [NB, C])
        c_silu = sb("c_silu", [NB, C])
        c_siluT = sb("c_siluT", [C, NB])
        wm_sb = sb("wm_sb", [C, 6 * C])
        mod = sb("mod", [C, 4, NB])
        g_sign = sb("g_sign", [NB, 2, C])
        g_raw = sb("g_raw", [NB, 2, C])
        g_size = sb("g_size", [NB, 2, C])

        x_in = two("x_in", [P, NT, C])
        x_res = two("x_res", [P, NT, C])
        gate_a = two("gate_a", [P, C])
        gate_b = two("gate_b", [P, C])
        stats = two("stats", [P, NT, 6])
        mean_var = two("mean_var", [P, NT, 2])
        var_eps = two("var_eps", [P, NT])
        rstd = two("rstd", [P, NT])
        xn = two("xn", [P, NT, C])
        hT = two("hT", [C, T])
        latT = two("latT", [P, P])
        q_parts = two("q_parts", [C, PARTS, T], BF16)
        q_rest = two("q_rest", [C, T])
        k_rest = two("k_rest", [KR, T])
        k_mid = two("k_mid", [KR, T], BF16)
        k_new = two("k_new", [MR, T], BF16)
        k_cur = two("k_cur", [P, T], BF16)
        v_new = two("v_new", [P, NT, HD])
        v_cur = two("v_cur", [P, 2, NT, VW])
        q_rows = two("q_rows", [P, NH, T], BF16)
        maxes = two("maxes", [P, NH, NT])
        max_rest = two("max_rest", [P, NH, NT])
        max_parts = two("max_parts", [P, PARTS, NH, NT], BF16)
        maxT = two("maxT", [PARTS * NH * NT, P], BF16)
        probs = [sb(f"probs{i}", [P, W]) for i in range(6)]
        y_raw = two("y_raw", [P, NC // 2, T])
        r_den = two("r_den", [P, NT * NH])
        y_tok = two("y_tok", [P, NT, C])
        yT = two("yT", [C, T])
        x_gated = two("x_gated", [P, NT, C])
        x_mid = two("x_mid", [P, NT, C])
        stats2 = two("stats2", [P, NT, 6])
        mean_var2 = two("mean_var2", [P, NT, 2])
        var_eps2 = two("var_eps2", [P, NT])
        rstd2 = two("rstd2", [P, NT])
        xn2 = two("xn2", [P, NT, C])
        h2T = two("h2T", [C, T])
        hidT = two("hidT", [P, P])
        logits = two("logits", [P, NT, NE])
        top = two("top", [P, NT])
        is_top = two("is_top", [P, NT, NE])
        top_rank = two("top_rank", [P, NT])
        ranked = two("ranked", [P, NT, NE])
        onehot = two("onehot", [P, NT, NE])
        chosen = two("chosen", [P, NT, NE, C])
        routed_g = two("routed_g", [P, NT, C])
        x_out = two("x_out", [P, NT, C])

        def bank(name):
            return ctx.enter_context(nc.psum_tensor(name, [P, W], F32))
        ps_s = [bank(f"ps_s{i}") for i in range(2)]
        ps_m = [bank(f"ps_m{i}") for i in range(2)]
        ps_y = bank("ps_y")
        ps_a = [bank(f"ps_a{i}") for i in range(2)]
        ps_b = bank("ps_b")

        ATTENTION_LOADS, ROUTER_LOADS = 5, 9
        cond_in = sem("cond_in")
        w_mod_in = sem("w_mod_in")
        attention_in = sem("attention_in")
        router_in = sem("router_in")
        gates_made = sem("gates_made")
        biases_ready = sem("biases_ready")
        consts_made = sem("consts_made")
        masks_made = sem("masks_made")
        mask_rows_in = sem("mask_rows_in")
        q_rows_zeroed = sem("q_rows_zeroed")
        be_zeroed = sem("be_zeroed")
        gps_step = sem("gps_step")
        setup_act = sem("setup_act")
        setup_dve = sem("setup_dve")
        setup_pe = sem("setup_pe")
        setup_ready = sem("setup_ready")
        setup_copy = sem("setup_copy")
        gates_out = sem("gates_out")
        x_in_loaded = [sem(f"x_in_loaded{i}") for i in range(2)]
        x_res_loaded = [sem(f"x_res_loaded{i}") for i in range(2)]
        gate_b_loaded = [sem(f"gate_b_loaded{i}") for i in range(2)]
        q_written = [sem(f"q_written{i}") for i in range(2)]
        q_loaded = [[sem(f"q_loaded{i}_{c}") for c in range(NC)] for i in range(2)]
        shift_loaded = [sem(f"shift_loaded{i}") for i in range(2)]
        out_stored = [sem(f"out_stored{i}") for i in range(2)]
        ln1_dve = sem("ln1_dve")
        ln1_rstd = sem("ln1_rstd")
        xnT_done = sem("xnT_done")
        hT_ready = sem("hT_ready")
        lat_done = sem("lat_done")
        latT_ready = sem("latT_ready")
        qk_done = sem("qk_done")
        qk_high = sem("qk_high")
        qk_dve = sem("qk_dve")
        qk_middle = sem("qk_middle")
        q_low = sem("q_low")
        v_done = sem("v_done")
        v_ready = sem("v_ready")
        max_scores = sem("max_scores")
        max_taken = sem("max_taken")
        max_split = sem("max_split")
        kv_moved = sem("kv_moved")
        maxT_done = sem("maxT_done")
        maxT_ready = sem("maxT_ready")
        scores_done = sem("scores_done")
        probs_ready = sem("probs_ready")
        pv_done = sem("pv_done")
        y_copied = sem("y_copied")
        y_turned = sem("y_turned")
        den_ready = sem("den_ready")
        y_normed = sem("y_normed")
        yT_done = sem("yT_done")
        yT_ready = sem("yT_ready")
        proj_done = sem("proj_done")
        x_mid_dve = sem("x_mid_dve")
        ln2_dve = sem("ln2_dve")
        ln2_rstd = sem("ln2_rstd")
        xn2T_done = sem("xn2T_done")
        h2T_ready = sem("h2T_ready")
        hid_done = sem("hid_done")
        hidT_ready = sem("hidT_ready")
        logits_done = sem("logits_done")
        route_dve = sem("route_dve")
        experts_done = sem("experts_done")
        expert_taken = sem("expert_taken")
        routed_gps = sem("routed_gps")
        out_ready = sem("out_ready")

        sp_went_on = sem("sp_went_on")
        dve_went_on = sem("dve_went_on")

        def steps(engine, step, after_first=lambda: None, after_second=lambda: None):
            first_pair, last_pair = 1, (NB - 4) // 2
            for i in range(-3, 2 * first_pair):
                step(Batch(0, i // 2, i % 2, NB))
                if i == -3:
                    after_first()
                if i == -2:
                    after_second()
            with engine.Fori(first_pair, last_pair) as pair:
                step(Batch(pair, 0, 0, NB))
                step(Batch(pair, 0, 1, NB))
            for i in range(2 * last_pair, NB + 2):
                step(Batch(0, i // 2, i % 2, NB))

        def score_chunk(c, kind):
            return (NC * c + 2 * kind, 2) if kind < 2 else (NC * c, 4)

        block = ctx.enter_context(nc.Block())

        @block.sync
        def _(sp):
            def load_x(b):
                src = x[bass.ds(b.index, 1), :, :].rearrange("a (n p) c -> p (a n) c", p=P)
                if b.at_least(2):
                    sp.wait_ge(ln1_dve, b.plus(-2).count(7, 7))
                    sp.sem_inc(sp_went_on, 1)
                sp.dma_start(x_in[b.parity][:, :, :], src).then_inc(x_in_loaded[b.parity], 16)

            def load(done, pairs):
                for dst, src in pairs:
                    sp.dma_start(dst, src).then_inc(done, 16)

            def halves(dst, src):
                return [(dst[64 * n:64 * n + 64, :], src) for n in range(NT)]

            assert LAT == HID == 64
            load(cond_in, [(c_sb[:, :], cond)])
            load(w_mod_in, [(wm_sb[:, :], w_mod)])
            load_x(Batch(0, 0, 0, NB))
            attention_loads = [(wd_sb[:, :], w_down)] + halves(wq_in, w_q) + halves(wkv_sb, w_kv)
            load(attention_in, attention_loads)
            load_x(Batch(0, 0, 1, NB))
            router_loads = halves(w2_in, w2) + halves(b1_sb, b1.rearrange("(m a) -> m a", a=1)) + [
                (be_rows[:, :], expert_b.rearrange("(a e) d -> a (e d)", a=1).broadcast_to([BR, NE * C])),
                (b2_sb[:, :], b2.rearrange("(a e) -> a e", a=1).broadcast_to([P, NE])),
                (wp_sb[:, :], w_proj), (w1_sb[:, :], w1),
                (we_sb[:, :].rearrange("h (e d) -> h e d", e=NE), expert_w.rearrange("e h d -> h e d"))]
            load(router_in, router_loads)
            assert len(attention_loads) == ATTENTION_LOADS and len(router_loads) == ROUTER_LOADS

            def step(i):
                fill, soft, done = i.plus(2), i, i.plus(-2)
                if i.plus(4).exists and i.at_least(-2):
                    load_x(i.plus(4))
                if soft.exists:
                    if soft.at_least(2):
                        sp.wait_ge(x_mid_dve, soft.plus(-2).count(2, 2))
                        sp.sem_inc(sp_went_on, 1)
                    sp.dma_start(x_res[soft.parity][:, :, :],
                                 x[bass.ds(soft.index, 1), :, :].rearrange("a (n p) c -> p (a n) c", p=P)
                                 ).then_inc(x_res_loaded[soft.parity], 16)
                    sp.dma_start(gate_a[soft.parity][:, :],
                                 gate_scratch[bass.ds(soft.index, 1), 0, :].broadcast_to([P, C])
                                 ).then_inc(x_res_loaded[soft.parity], 16)
                if fill.exists:
                    sp.wait_ge(qk_middle, fill.count(2, 1))
                    sp.sem_inc(sp_went_on, 1)
                    sp.wait_ge(q_low, fill.count(1, 1))
                    if fill.at_least(2):
                        for c in range(NC):
                            sp.wait_ge(q_loaded[fill.parity][c], fill.plus(-2).pair_count(48, 48))
                    for pq in range(PARTS):
                        sp.dma_start(
                            q_scratch[fill.parity, pq * HD:(pq + 1) * HD, :, :].rearrange("d h t -> h d t"),
                            q_parts[fill.parity][:, pq, :]).then_inc(q_written[fill.parity], 16)
                    if isinstance(fill.pair, int) and not fill.at_least(2):
                        sp.wait_ge(q_rows_zeroed, fill.index + 1)
                        for dst in (k_new[fill.parity], k_cur[fill.parity]):
                            sp.dma_start(dst[KR:MR, :], key_block[:, :]).then_inc(mask_rows_in, 16)
                        sp.dma_start(q_rows[fill.parity][KR:MR, :, :],
                                     before_block[:, :].unsqueeze(1).broadcast_to([PIECES, NH, T])
                                     ).then_inc(mask_rows_in, 16)
                    sp.wait_ge(q_written[fill.parity], fill.pair_count(48, 48))
                    sp.sem_inc(sp_went_on, 1)
                    for c in range(NC):
                        if soft.exists:
                            sp.wait_ge(scores_done, soft.count(CH, 3 * c + 3))
                        for pk in range(PARTS):
                            sp.dma_start(q_rows[fill.parity][32 * pk:32 * pk + QR, 4 * c:4 * c + 4, :],
                                         q_scratch[fill.parity, :, 4 * c:4 * c + 4, :]
                                         ).then_inc(q_loaded[fill.parity][c], 16)
                if done.exists:
                    sp.wait_ge(out_ready, done.count(NT, NT))
                    sp.sem_inc(sp_went_on, 1)
                    sp.dma_start(out[bass.ds(done.index, 1), :, :].rearrange("a (n p) c -> p (a n) c", p=P),
                                 x_out[done.parity][:, :, :]).then_inc(out_stored[done.parity], 16)
                if soft.exists:
                    sp.dma_start(gate_b[soft.parity][:, :],
                                 gate_scratch[bass.ds(soft.index, 1), 1, :].broadcast_to([P, C])
                                 ).then_inc(gate_b_loaded[soft.parity], 16)

            sp.wait_ge(gates_made, 1)
            sp.dma_start(gate_scratch, g_size[:, :, :]).then_inc(gates_out, 16)
            sp.wait_ge(gates_out, 16)
            steps(sp, step)
            for par in range(2):
                sp.wait_ge(out_stored[par], 16 * NB // 2)

        @block.gpsimd
        def _(gp):
            k = [0]

            def made(ins):
                k[0] += 1
                ins.then_inc(gps_step, 1)
                gp.wait_ge(gps_step, k[0])

            made(gp.memset(ident[:, :], 0.0))
            made(gp.affine_select(out=ident[:, :], in_=ident[:, :], compare_op=ALU.not_equal, fill=1.0, base=0,
                                  pattern=[[-1, P]], channel_multiplier=1))
            gp.tensor_copy(ident_b[:, :], ident[:, :]).then_inc(consts_made, 1)
            gp.memset(minus_half[:, :], -0.5).then_inc(gps_step, 1)
            k[0] += 1

            def masks_and_rows():
                gp.wait_ge(gps_step, k[0])
                made(gp.memset(key_block[:, :], 1.0))
                made(gp.affine_select(out=key_block[:, :], in_=key_block[:, :], compare_op=ALU.is_ge, fill=0.0, base=0,
                                      pattern=[[1, T]], channel_multiplier=-PIECE))
                made(gp.affine_select(out=key_block[:, :], in_=key_block[:, :], compare_op=ALU.is_ge, fill=0.0,
                                      base=PIECE - 1, pattern=[[-1, T]], channel_multiplier=PIECE))
                made(gp.memset(before_block[:, :], NEG))
                made(gp.affine_select(out=before_block[:, :], in_=before_block[:, :], compare_op=ALU.is_ge, fill=0.0,
                                      base=-1, pattern=[[-1, T]], channel_multiplier=PIECE))
                made(gp.memset(future[:, :], 0.0))
                made(gp.memset(later[:, :], 0.0))
                made(gp.affine_select(out=future[:, :], in_=future[:, :], compare_op=ALU.is_ge, fill=NEG, base=0,
                                      pattern=[[-1, P]], channel_multiplier=1))
                gp.affine_select(out=later[:, :], in_=later[:, :], compare_op=ALU.is_ge, fill=NEG, base=0,
                                 pattern=[[1, P]], channel_multiplier=-1).then_inc(masks_made, 1)
                gp.memset(q_rows[0][:, :, :], 0.0).then_inc(q_rows_zeroed, 1)

            def bias_rows_and_rows():
                gp.wait_ge(masks_made, 1)
                gp.memset(be_parts[:, :], 0.0).then_inc(be_zeroed, 1)
                gp.wait_ge(be_zeroed, 1)
                made(gp.memset(pick3[:, :], 0.0))
                for p in range(PARTS):
                    made(gp.memset(pick3[32 * p:32 * p + 1, :], 1.0))
                gp.memset(q_rows[1][:, :, :], 0.0).then_inc(q_rows_zeroed, 1)

            def power(dst, src):
                return gp.tensor_tensor(dst, src, minus_half[:, :], ALU.pow)

            def step(i):
                norm, fill, end, done = i.plus(3), i.plus(2), i.plus(-1), i.plus(-2)
                for s in range(CH):
                    if s == AT["rstd_mid"] and end.exists:
                        gp.wait_ge(ln2_dve, end.count(7, 5))
                        power(rstd2[end.parity][:, :], var_eps2[end.parity][:, :]).then_inc(ln2_rstd, 1)
                    if s == AT["low_q"] and fill.exists:
                        gp.wait_ge(qk_middle, fill.count(2, 1))
                        gp.tensor_tensor(q_parts[fill.parity][:, 2, :], q_rest[fill.parity][:, :],
                                         q_parts[fill.parity][:, 1, :], ALU.subtract).then_inc(q_low, 1)
                    if s == AT["rstd_x"] and norm.exists:
                        gp.wait_ge(ln1_dve, norm.count(7, 5))
                        power(rstd[norm.parity][:, :], var_eps[norm.parity][:, :]).then_inc(ln1_rstd, 1)
                    if s in AT["sum_experts"] and done.exists:
                        t = AT["sum_experts"].index(s)
                        gp.wait_ge(expert_taken, done.count(2 * NT, 2 * t + 2))
                        ch = chosen[done.parity]
                        half, k = NE // 2, 0
                        while half:
                            gp.tensor_tensor(ch[:, t, 0:half, :], ch[:, t, 0:half, :], ch[:, t, half:2 * half, :],
                                             ALU.add).then_inc(routed_gps, 1)
                            half, k = half // 2, k + 1
                            gp.wait_ge(routed_gps, done.count(8, 4 * t + k))
                        if t == 0:
                            gp.wait_ge(gate_b_loaded[done.parity], done.pair_count(16, 16))
                        gp.tensor_tensor(routed_g[done.parity][:, t, :], ch[:, t, 0, :],
                                         gate_b[done.parity][:, :], ALU.mult).then_inc(routed_gps, 1)
                        gp.wait_ge(routed_gps, done.count(8, 4 * t + 4))
                        if done.at_least(2):
                            gp.wait_ge(out_stored[done.parity], done.plus(-2).pair_count(16, 16))
                        gp.tensor_tensor(x_out[done.parity][:, t, :], routed_g[done.parity][:, t, :],
                                         x_mid[done.parity][:, t, :], ALU.add).then_inc(out_ready, 1)

            gp.wait_ge(gps_step, k[0])
            steps(gp, step, masks_and_rows, bias_rows_and_rows)

        @block.scalar
        def _(act):
            act.wait_ge(cond_in, 16)
            nc.scalar.activation(c_exp[:, :], c_sb[:, :], ACT.Exp, scale=-1.0).then_inc(setup_act, 1)
            act.wait_ge(setup_ready, 1)

            def step(i):
                fill, maxi, soft, end = i.plus(2), i.plus(1), i, i.plus(-1)
                for s in range(CH):
                    if soft.exists:
                        act.wait_ge(scores_done, soft.count(CH, s + 1))
                        if s >= 6 or soft.at_least(1):
                            act.wait_ge(pv_done, soft.count(NC, s // 3 - 1))
                        nc.scalar.activation(probs[s % 6][:, :], ps_s[s % 2][:, :], ACT.Exp,
                                             scale=SCALE).then_inc(probs_ready, 1)
                    if s == AT["turn_x"] and fill.exists:
                        act.wait_ge(xnT_done, fill.count(1, 1))
                        nc.scalar.activation(hT[fill.parity][:, :], ps_b[:, 0:T], ACT.Identity,
                                             bias=mod[:, 0, bass.ds(fill.index, 1)],
                                             scale=mod[:, 1, bass.ds(fill.index, 1)]).then_inc(hT_ready, 1)
                    if s == AT["last_values"] and end.exists:
                        act.wait_ge(pv_done, end.count(NC, NC))
                        nc.scalar.activation(y_raw[end.parity][:, :, :],
                                             ps_y[:, :].rearrange("p (c t) -> p c t", c=2), ACT.Copy
                                             ).then_inc(y_copied, 1)
                    if s == AT["latent"] and fill.exists:
                        act.wait_ge(lat_done, fill.count(1, 1))
                        nc.scalar.activation(latT[fill.parity][:, :], ps_b[:, 0:P], ACT.Copy
                                             ).then_inc(latT_ready, 1)
                    if s == AT["qk"] and fill.exists:
                        act.wait_ge(qk_done, fill.count(1, 1))
                        if fill.at_least(2):
                            act.wait_ge(q_written[fill.parity], fill.plus(-2).pair_count(48, 48))
                        nc.scalar.activation(q_parts[fill.parity][:, 0, :], ps_b[:, 0:T], ACT.Copy
                                             ).then_inc(qk_high, 1)
                        nc.scalar.activation(k_new[fill.parity][0:KR, :], ps_b[0:KR, T:2 * T], ACT.Copy
                                             ).then_inc(qk_high, 1)
                    if s == AT["middle_qk"] and fill.exists:
                        par = fill.parity
                        act.wait_ge(qk_dve, fill.count(4, 2))
                        nc.scalar.activation(q_parts[par][:, 1, :], q_rest[par][:, :], ACT.Copy
                                             ).then_inc(qk_middle, 1)
                        nc.scalar.activation(k_new[par][32:64, :], k_rest[par][32:64, :], ACT.Copy
                                             ).then_inc(qk_middle, 1)
                    if s == AT["move_kv"] and maxi.exists:
                        par = maxi.parity
                        act.wait_ge(v_ready, maxi.count(1, 1))
                        act.wait_ge(qk_middle, maxi.count(2, 2))
                        act.wait_ge(qk_dve, maxi.count(4, 4))
                        if maxi.at_least(2):
                            act.wait_ge(pv_done, maxi.plus(-2).count(NC, NC))
                        nc.scalar.activation(k_cur[par][0:KR, :], k_new[par][0:KR, :], ACT.Copy).then_inc(kv_moved, 1)
                        for u in range(2):
                            nc.scalar.activation(v_cur[par][:, u, :, HW * u:HW * u + HD], v_new[par][:, :, :],
                                                 ACT.Copy).then_inc(kv_moved, 1)
                    if s == AT["turn_y_back"] and end.exists:
                        act.wait_ge(yT_done, end.count(1, 1))
                        nc.scalar.activation(yT[end.parity][:, :], ps_b[:, 0:T], ACT.Copy).then_inc(yT_ready, 1)
                    if s == AT["v"] and fill.exists:
                        act.wait_ge(v_done, fill.count(1, 1))
                        nc.scalar.activation(v_new[fill.parity][:, :, :],
                                             ps_b[:, 0:NT * HD].rearrange("p (n d) -> p n d", n=NT), ACT.Copy
                                             ).then_inc(v_ready, 1)
                    if s == AT["turn_max"] and maxi.exists:
                        act.wait_ge(maxT_done, maxi.count(1, 1))
                        nc.scalar.activation(maxT[maxi.parity][:, :],
                                             ps_a[MAXT_BANK][0:PARTS * NH * NT, 0:P // 2].bitcast(BF16), ACT.Copy
                                             ).then_inc(maxT_ready, 1)
                    if s == AT["turn_mid"] and end.exists:
                        act.wait_ge(xn2T_done, end.count(1, 1))
                        nc.scalar.activation(h2T[end.parity][:, :], ps_b[:, 0:T], ACT.Identity,
                                             bias=mod[:, 2, bass.ds(end.index, 1)],
                                             scale=mod[:, 3, bass.ds(end.index, 1)]).then_inc(h2T_ready, 1)
                    if s == AT["turn_max"] and maxi.exists:
                        act.wait_ge(maxT_ready, maxi.count(1, 1))
                        act.dma_start(q_rows[maxi.parity][MR:KRS, :, :], maxT[maxi.parity][:, :]
                                      ).then_inc(shift_loaded[maxi.parity], 16)
                    if s == AT["hidden"] and end.exists:
                        act.wait_ge(hid_done, end.count(1, 1))
                        nc.scalar.activation(hidT[end.parity][:, :], ps_b[:, 0:P], ACT.Relu,
                                             bias=b1_sb[:, :]).then_inc(hidT_ready, 1)

            steps(act, step, after_second=lambda: act.wait_ge(router_in, 16 * ROUTER_LOADS))

        @block.vector
        def _(dve):
            n = [0]

            def then(ins):
                n[0] += 1
                ins.then_inc(setup_dve, 1)
                dve.wait_ge(setup_dve, n[0])

            V = nc.vector
            for e in range(NE):
                V.memset(rank[:, e:e + 1], float(NE - e))
            for par in range(2):
                V.memset(v_cur[par][:, :, :, :], 0.0)
                V.memset(k_cur[par][KR:KR + 32, :], -1.0)
            V.memset(wq_sb[:, :, :], 0.0)
            V.memset(wk_rep[:, :, :], 0.0)
            V.memset(wv_two[:, :], 0.0)
            then(V.memset(w2_two[:, :], 0.0))
            for par in range(2):
                for u in range(2):
                    V.memset(v_cur[par][:, u, :, HW * u + HD:HW * u + HD + 1], 1.0)
            dve.wait_ge(setup_act, 1)
            then(V.tensor_scalar(c_exp[:, :], c_exp[:, :], 1.0, None, ALU.add))
            then(V.reciprocal(c_exp[:, :], c_exp[:, :]))
            V.tensor_tensor(c_silu[:, :], c_sb[:, :], c_exp[:, :], ALU.mult).then_inc(setup_copy, 1)
            dve.wait_ge(setup_pe, 1)
            V.tensor_copy(c_siluT[:, :], ps_a[0][:, 0:NB]).then_inc(setup_copy, 1)
            dve.wait_ge(attention_in, 16 * ATTENTION_LOADS)
            for t in range(NT):
                half = slice(64 * t, 64 * t + 64)
                for r in range(2):
                    V.tensor_copy(
                        wq_sb[half, t, r * 64:r * 64 + 64].rearrange("l (u j d) -> l u j d", u=2, j=4),
                        wq_in[half, r * 64:r * 64 + 64].rearrange("l (j u d) -> l u j d", u=2, j=4))
                for pk in range(PARTS):
                    V.tensor_copy(wk_rep[half, t, 32 * pk:32 * pk + QR].rearrange("l (a d) -> l a d", a=PARTS),
                                  wkv_sb[half, 0:HD].unsqueeze(1).broadcast_to([64, PARTS, HD]))
                V.tensor_copy(wv_two[half, t * HD:(t + 1) * HD], wkv_sb[half, HD:2 * HD])
            dve.wait_ge(setup_pe, 2)
            for m in range(4):
                last = V.tensor_scalar(mod[:, m, :], ps_a[0][:, 64 * m:64 * m + NB], float(m % 2), None, ALU.add)
            last.then_inc(setup_ready, 1)

            def make_gates():
                gv = ps_m[0][0:NB, 0:2 * C].rearrange("b (g c) -> b g c", g=2)
                then(V.tensor_scalar(g_sign[:, :, :], gv, 0.0, 2.0, ALU.is_ge, ALU.mult))
                then(V.tensor_copy(g_raw[:, :, :], gv))
                then(V.scalar_tensor_tensor(g_size[:, :, :], g_raw[:, :, :], -1.0, g_raw[:, :, :],
                                            ALU.mult, ALU.max))
                then(V.tensor_scalar(g_size[:, :, :], g_size[:, :, :], 0.25, None, ALU.max))
                V.scalar_tensor_tensor(g_size[:, :, :], g_sign[:, :, :], -1.0, g_size[:, :, :],
                                       ALU.add, ALU.mult).then_inc(gates_made, 1)
                dve.wait_ge(router_in, 16 * ROUTER_LOADS)
                for t in range(NT):
                    half = slice(64 * t, 64 * t + 64)
                    V.tensor_copy(w2_two[half, t * NE:(t + 1) * NE], w2_in[half, :])

            def split_biases():
                dve.wait_ge(be_zeroed, 1)
                then(V.tensor_copy(be_hi[:, :], be_rows[:, :]))
                then(V.tensor_tensor(be_rest[:, :], be_rows[:, :], be_hi[:, :], ALU.subtract))
                V.tensor_copy(be_parts[0:1, :], be_rows[0:1, :])
                V.tensor_copy(be_parts[32:33, :], be_rest[32:33, :])
                then(V.tensor_copy(be_mid[64:65, :], be_rest[64:65, :]))
                V.tensor_tensor(be_parts[64:65, :], be_rest[64:65, :], be_mid[64:65, :], ALU.subtract
                                ).then_inc(biases_ready, 1)

            def norm_stats(src, st, mv, ve, done, b):
                for t in range(NT):
                    V.bn_stats(st[:, t, :], src[:, t, :]).then_inc(done, 1)
                dve.wait_ge(done, b.count(7, 2))
                dve.sem_inc(dve_went_on, 1)
                for t in range(NT):
                    V.bn_aggr(mv[:, t, :], st[:, t, :]).then_inc(done, 1)
                dve.wait_ge(done, b.count(7, 4))
                V.tensor_scalar(ve[:, :], mv[:, :, 1], EPS, None, ALU.add).then_inc(done, 1)

            def norm_apply(dst, src, mv, rs, done):
                for t in range(NT):
                    V.tensor_scalar(dst[:, t, :], src[:, t, :], mv[:, t, 0:1], rs[:, t:t + 1],
                                    ALU.subtract, ALU.mult).then_inc(done, 1)

            def take_max(b, m):
                c, kind = m // 3, m % 3
                h0, heads = score_chunk(c, kind)
                dve.wait_ge(max_scores, b.count(CH, m + 1))
                V.tensor_reduce(maxes[b.parity][:, h0:h0 + heads, 1 if kind < 2 else 0],
                                ps_m[m % 2][:, :].rearrange("p (h s) -> p h s", h=heads),
                                AX.X, ALU.max).then_inc(max_taken, 1)

            def take_expert(b, n):
                t, half = n // 2, n % 2
                dve.wait_ge(experts_done, b.count(2 * NT, n + 1))
                if n == 0:
                    dve.wait_ge(route_dve, b.count(6, 6))
                V.tensor_tensor(chosen[b.parity][:, t, half * EB:(half + 1) * EB, :],
                                ps_a[n % 2][:, :].rearrange("p (e c) -> p e c", e=EB),
                                onehot[b.parity][:, t, half * EB:(half + 1) * EB].unsqueeze(2).broadcast_to(
                                    [P, EB, C]), ALU.mult).then_inc(expert_taken, 1)

            def step(i):
                norm, fill, maxi, soft, end, done = i.plus(3), i.plus(2), i.plus(1), i, i.plus(-1), i.plus(-2)
                for s in range(CH):
                    if s == AT["route"] and done.exists:
                        par = done.parity
                        dve.wait_ge(logits_done, done.count(1, 1))
                        V.tensor_tensor(logits[par][:, :, :],
                                        ps_b[:, 0:NT * NE].rearrange("p (n e) -> p n e", n=NT),
                                        b2_sb[:, :].unsqueeze(1).broadcast_to([P, NT, NE]), ALU.add
                                        ).then_inc(route_dve, 1)
                        dve.wait_ge(route_dve, done.count(6, 1))
                        V.tensor_reduce(top[par][:, :], logits[par][:, :, :], AX.X, ALU.max
                                        ).then_inc(route_dve, 1)
                        dve.wait_ge(route_dve, done.count(6, 2))
                        V.tensor_tensor(is_top[par][:, :, :], logits[par][:, :, :],
                                        top[par][:, :].unsqueeze(2).broadcast_to([P, NT, NE]),
                                        ALU.is_equal).then_inc(route_dve, 1)
                        dve.wait_ge(route_dve, done.count(6, 3))
                        V.tensor_tensor(ranked[par][:, :, :], is_top[par][:, :, :],
                                        rank[:, :].unsqueeze(1).broadcast_to([P, NT, NE]), ALU.mult
                                        ).then_inc(route_dve, 1)
                        dve.wait_ge(route_dve, done.count(6, 4))
                        V.tensor_reduce(top_rank[par][:, :], ranked[par][:, :, :], AX.X, ALU.max
                                        ).then_inc(route_dve, 1)
                        dve.wait_ge(route_dve, done.count(6, 5))
                        V.tensor_tensor(onehot[par][:, :, :], ranked[par][:, :, :],
                                        top_rank[par][:, :].unsqueeze(2).broadcast_to([P, NT, NE]), ALU.is_equal
                                        ).then_inc(route_dve, 1)
                    if s == AT["normalise_y"] and end.exists:
                        dve.wait_ge(y_turned, end.count(1, 1))
                        turned = ps_b[:, :].rearrange("p (h w) -> p h w", w=HW)
                        V.reciprocal(r_den[end.parity][:, :], turned[:, :, HD]).then_inc(den_ready, 1)
                        dve.wait_ge(den_ready, end.count(1, 1))
                        V.tensor_tensor(y_tok[end.parity][:, :, :].rearrange("p n (h d) -> p (n h) d", d=HD),
                                        turned[:, :, 0:HD],
                                        r_den[end.parity][:, :].unsqueeze(2).broadcast_to([P, NT * NH, HD]),
                                        ALU.mult).then_inc(y_normed, 1)
                    if s == AT["split_qk"] and fill.exists:
                        par = fill.parity
                        dve.wait_ge(qk_high, fill.count(2, 2))
                        V.tensor_tensor(q_rest[par][:, :], ps_b[:, 0:T], q_parts[par][:, 0, :],
                                        ALU.subtract).then_inc(qk_dve, 1)
                        V.tensor_tensor(k_rest[par][:, :], ps_b[0:KR, T:2 * T], k_new[par][0:KR, :],
                                        ALU.subtract).then_inc(qk_dve, 1)
                        dve.wait_ge(qk_dve, fill.count(4, 2))
                        V.tensor_copy(k_mid[par][64:96, :], k_rest[par][64:96, :]).then_inc(qk_dve, 1)
                        dve.wait_ge(qk_dve, fill.count(4, 3))
                        V.tensor_tensor(k_new[par][64:96, :], k_rest[par][64:96, :], k_mid[par][64:96, :],
                                        ALU.subtract).then_inc(qk_dve, 1)
                    if s == AT["middle"] and end.exists:
                        par = end.parity
                        dve.wait_ge(proj_done, end.count(1, 1))
                        dve.wait_ge(x_res_loaded[par], end.pair_count(32, 32))
                        V.tensor_tensor(x_gated[par][:, :, :], ps_b[:, 0:T].rearrange("p (n c) -> p n c", n=NT),
                                        gate_a[par][:, :].unsqueeze(1).broadcast_to([P, NT, C]), ALU.mult
                                        ).then_inc(x_mid_dve, 1)
                        dve.wait_ge(x_mid_dve, end.count(2, 1))
                        if end.at_least(2):
                            dve.wait_ge(out_ready, end.plus(-2).count(NT, NT))
                        V.tensor_tensor(x_mid[par][:, :, :], x_gated[par][:, :, :], x_res[par][:, :, :],
                                        ALU.add).then_inc(x_mid_dve, 1)
                        dve.wait_ge(x_mid_dve, end.count(2, 2))
                        norm_stats(x_mid[par], stats2[par], mean_var2[par], var_eps2[par], ln2_dve, end)
                    if s == AT["split_max"] and maxi.exists:
                        par = maxi.parity
                        dve.wait_ge(max_taken, maxi.count(CH, CH))
                        V.tensor_copy(max_parts[par][:, 0, :, :], maxes[par][:, :, :]).then_inc(max_split, 1)
                        dve.wait_ge(max_split, maxi.count(4, 1))
                        V.tensor_tensor(max_rest[par][:, :, :], maxes[par][:, :, :], max_parts[par][:, 0, :, :],
                                        ALU.subtract).then_inc(max_split, 1)
                        dve.wait_ge(max_split, maxi.count(4, 2))
                        V.tensor_copy(max_parts[par][:, 1, :, :], max_rest[par][:, :, :]).then_inc(max_split, 1)
                        dve.wait_ge(max_split, maxi.count(4, 3))
                        V.tensor_tensor(max_parts[par][:, 2, :, :], max_rest[par][:, :, :],
                                        max_parts[par][:, 1, :, :], ALU.subtract).then_inc(max_split, 1)
                    if s == AT["norm_mid"] and end.exists:
                        dve.wait_ge(ln2_rstd, end.count(1, 1))
                        norm_apply(xn2[end.parity], x_mid[end.parity], mean_var2[end.parity],
                                   rstd2[end.parity], ln2_dve)
                    if s == AT["stats_x"] and norm.exists:
                        dve.wait_ge(x_in_loaded[norm.parity], norm.pair_count(16, 16))
                        norm_stats(x_in[norm.parity], stats[norm.parity], mean_var[norm.parity],
                                   var_eps[norm.parity], ln1_dve, norm)
                    if s == AT["norm_x"] and norm.exists:
                        dve.wait_ge(ln1_rstd, norm.count(1, 1))
                        norm_apply(xn[norm.parity], x_in[norm.parity], mean_var[norm.parity],
                                   rstd[norm.parity], ln1_dve)
                    for n in range(2 * NT):
                        if s == AT["take_experts"][n] and done.exists:
                            take_expert(done, n)
                    if maxi.exists:
                        for m in range(MAX_FROM[s], MAX_FROM[s] + MAX_CHUNKS[s]):
                            take_max(maxi, m)

            steps(dve, step, make_gates, split_biases)

        @block.tensor
        def _(pe):
            MM, TR = nc.tensor.matmul, nc.tensor.transpose
            pe.wait_ge(setup_copy, 1)
            pe.wait_ge(consts_made, 1)
            TR(ps_a[0][:, 0:NB], c_silu[:, :], ident[0:NB, 0:NB]).then_inc(setup_pe, 1)
            pe.wait_ge(setup_copy, 2)
            pe.wait_ge(w_mod_in, 16)
            for m, part in enumerate((0, 1, 3, 4)):
                MM(ps_a[0][:, 64 * m:64 * m + NB], wm_sb[:, part * C:(part + 1) * C], c_siluT[:, :],
                   start=True, stop=True)
            MM(ps_m[0][0:NB, 0:C], c_siluT[:, :], wm_sb[:, 2 * C:3 * C], start=True, stop=True)
            MM(ps_m[0][0:NB, C:2 * C], c_siluT[:, :], wm_sb[:, 5 * C:6 * C], start=True, stop=True
               ).then_inc(setup_pe, 1)
            pe.wait_ge(setup_ready, 1)

            def mask_diagonal(bk, mask, heads):
                for at in range(0, P, PIECE):
                    piece = slice(at, at + PIECE)
                    last = MM(bk[piece, :, piece], ident_b[:, piece],
                              mask[:, piece].unsqueeze(1).broadcast_to([P, heads, PIECE]), start=False, stop=True,
                              tile_position=(0, at), skip_group_check=True)
                return last

            def scores(b, s):
                c, kind = s // 3, s % 3
                h0, heads = score_chunk(c, kind)
                if s == 0:
                    pe.wait_ge(kv_moved, b.count(3, 3))
                    pe.wait_ge(shift_loaded[b.parity], b.pair_count(16, 16))
                if s >= 2 or b.at_least(1):
                    pe.wait_ge(probs_ready, b.count(CH, s - 1))
                q = q_rows[b.parity][0:KRS, h0:h0 + heads, :]
                key_tile, q = (0, q) if kind < 2 else (1, q[:, :, P:T])
                MM(ps_s[s % 2][:, :], k_cur[b.parity][0:KRS, key_tile * P:(key_tile + 1) * P], q,
                   start=True, stop=True)
                mask_diagonal(ps_s[s % 2][:, :].rearrange("p (h t) -> p h t", h=heads)[:, :, 0:P], later, heads
                              ).then_inc(scores_done, 1)

            def max_scores_of(b, m):
                c, kind = m // 3, m % 3
                h0, heads = score_chunk(c, kind)
                if m == 0:
                    pe.wait_ge(qk_dve, b.count(4, 4))
                    pe.wait_ge(qk_middle, b.count(2, 2))
                    if isinstance(b.pair, int) and not b.at_least(2):
                        pe.wait_ge(mask_rows_in, 48 * (b.index + 1))
                if kind == 0:
                    pe.wait_ge(q_loaded[b.parity][c], b.pair_count(48, 48))
                if m >= 2 or b.at_least(1):
                    pe.wait_ge(max_taken, b.count(CH, m - 1))
                bk = ps_m[m % 2]
                tile = 1 if kind < 2 else 0
                keys = P * (tile + 1)
                for n in range(heads):
                    MM(bk[:, n * keys:(n + 1) * keys], q_rows[b.parity][0:MR, h0 + n, tile * P:(tile + 1) * P],
                       k_new[b.parity][0:MR, 0:keys], start=(n == 0), stop=(n == heads - 1), skip_group_check=True)
                mask_diagonal(bk[:, :].rearrange("p (h s) -> p h s", h=heads)[:, :, tile * P:keys], future, heads
                              ).then_inc(max_scores, 1)

            def values(b, c):
                pe.wait_ge(probs_ready, b.count(CH, 3 * c + 3))
                if c == 0 and b.at_least(1):
                    pe.wait_ge(y_copied, b.count(1, 0))
                r, u = c // 2, c % 2
                v = v_cur[b.parity]
                at = r * T
                for j in range(4):
                    p = probs[(3 * c + j // 2) % 6]
                    MM(ps_y[32 * j:32 * j + VW, at:at + T], v[:, u, 0, :], p[:, (j % 2) * T:(j % 2 + 1) * T],
                       start=(u == 0), stop=False, tile_position=(0, 32 * j))
                p = probs[(3 * c + 2) % 6]
                for j in range(4):
                    last = MM(ps_y[32 * j:32 * j + VW, at + P:at + T], v[:, u, 1, :], p[:, j * P:(j + 1) * P],
                              start=False, stop=(u == 1), tile_position=(0, 32 * j))
                last.then_inc(pv_done, 1)

            def step(i):
                fill, maxi, soft, end, done = i.plus(2), i.plus(1), i, i.plus(-1), i.plus(-2)
                for s in range(CH):
                    if soft.exists:
                        scores(soft, s)
                    if s == AT["last_values"] and end.exists:
                        values(end, NC - 1)
                    if s == AT["logits"] and done.exists:
                        pe.wait_ge(hidT_ready, done.count(1, 1))
                        MM(ps_b[:, 0:NT * NE], hidT[done.parity][:, :], w2_two[:, :], start=True, stop=True
                           ).then_inc(logits_done, 1)
                    if s == AT["turn_y"] and end.exists:
                        pe.wait_ge(y_copied, end.count(1, 1))
                        if done.exists:
                            pe.wait_ge(route_dve, done.count(6, 1))
                        elif soft.exists:
                            pe.wait_ge(v_ready, maxi.count(1, 1))
                        for t in range(NT):
                            for r in range(NC // 2):
                                last = TR(ps_b[:, (2 * t + r) * P:(2 * t + r + 1) * P],
                                          y_raw[end.parity][:, r, t * P:(t + 1) * P], ident[:, :])
                        last.then_inc(y_turned, 1)
                    if s == AT["turn_x"] and fill.exists:
                        pe.wait_ge(ln1_dve, fill.count(7, 7))
                        if end.exists:
                            pe.wait_ge(y_normed, end.count(1, 1))
                        elif fill.at_least(1):
                            pe.wait_ge(v_ready, fill.count(1, 0))
                        for t in range(NT):
                            last = TR(ps_b[:, t * P:(t + 1) * P], xn[fill.parity][:, t, :], ident[:, :])
                        last.then_inc(xnT_done, 1)
                    if s == AT["turn_y_back"] and end.exists:
                        if fill.exists:
                            pe.wait_ge(hT_ready, fill.count(1, 1))
                        pe.wait_ge(y_normed, end.count(1, 1))
                        for t in range(NT):
                            last = TR(ps_b[:, t * P:(t + 1) * P], y_tok[end.parity][:, t, :], ident[:, :])
                        last.then_inc(yT_done, 1)
                    if s == AT["project"] and end.exists:
                        pe.wait_ge(yT_ready, end.count(1, 1))
                        for t in range(NT):
                            last = MM(ps_b[:, t * P:(t + 1) * P], yT[end.parity][:, t * P:(t + 1) * P], wp_sb[:, :],
                                      start=True, stop=True)
                        last.then_inc(proj_done, 1)
                    if s == AT["qk"] and fill.exists:
                        pe.wait_ge(latT_ready, fill.count(1, 1))
                        for at, rows, w in ((0, C, wq_sb), (T, KR, wk_rep)):
                            for t in range(NT):
                                last = MM(ps_b[0:rows, at + t * P:at + (t + 1) * P], w[:, t, :],
                                          latT[fill.parity][:, :], start=True, stop=True)
                        last.then_inc(qk_done, 1)
                    if s == AT["v"] and fill.exists:
                        pe.wait_ge(qk_dve, fill.count(4, 2))
                        MM(ps_b[:, 0:NT * HD], latT[fill.parity][:, :], wv_two[:, :], start=True, stop=True
                           ).then_inc(v_done, 1)
                    if s == AT["turn_mid"] and end.exists:
                        pe.wait_ge(ln2_dve, end.count(7, 7))
                        if fill.exists:
                            pe.wait_ge(v_ready, fill.count(1, 1))
                        for t in range(NT):
                            last = TR(ps_b[:, t * P:(t + 1) * P], xn2[end.parity][:, t, :], ident[:, :])
                        last.then_inc(xn2T_done, 1)
                    if s == AT["hidden"] and end.exists:
                        pe.wait_ge(h2T_ready, end.count(1, 1))
                        for t in range(NT):
                            last = MM(ps_b[HID * t:HID * (t + 1), 0:P], w1_sb[:, :],
                                      h2T[end.parity][:, t * P:(t + 1) * P], start=True, stop=True,
                                      tile_position=(0, HID * t))
                        last.then_inc(hid_done, 1)
                    if s in AT["experts"] and done.exists:
                        n = AT["experts"].index(s)
                        t, half = n // 2, n % 2
                        if (n > 0 or not end.exists) and (n > 1 or done.at_least(1)):
                            pe.wait_ge(expert_taken, done.count(2 * NT, n - 1))
                        if n == EXPERTS_BEFORE and maxi.exists:
                            pe.wait_ge(maxT_ready, maxi.count(1, 1))
                        if n == 0 and EXPERTS_BEFORE == 2 * NT and soft.exists:
                            pe.wait_ge(maxT_ready, soft.count(1, 1))
                        MM(ps_a[n % 2][:, :], pick3[:, :], be_parts[:, half * W:(half + 1) * W], start=True, stop=False)
                        MM(ps_a[n % 2][:, :], h2T[done.parity][:, t * P:(t + 1) * P],
                           we_sb[:, half * W:(half + 1) * W], start=False, stop=True
                           ).then_inc(experts_done, 1)
                    if s == AT["turn_max"] and maxi.exists:
                        pe.wait_ge(max_split, maxi.count(4, 4))
                        if done.exists and EXPERTS_BEFORE > 1:
                            pe.wait_ge(expert_taken, done.count(2 * NT, EXPERTS_BEFORE - 1))
                        TR(ps_a[MAXT_BANK][0:PARTS * NH * NT, 0:P // 2].bitcast(BF16),
                           max_parts[maxi.parity][:, :, :, :].rearrange("p a h n -> p (a h n)"), ident_b[:, :]
                           ).then_inc(maxT_done, 1)
                    if maxi.exists:
                        for m in range(MAX_FROM[s], MAX_FROM[s] + MAX_CHUNKS[s]):
                            max_scores_of(maxi, m)
                    if s == AT["latent"] and fill.exists:
                        pe.wait_ge(hT_ready, fill.count(1, 1))
                        if end.exists:
                            pe.wait_ge(x_mid_dve, end.count(2, 1))
                        for t in range(NT):
                            last = MM(ps_b[LAT * t:LAT * (t + 1), 0:P], wd_sb[:, :],
                                      hT[fill.parity][:, t * P:(t + 1) * P], start=True, stop=True,
                                      tile_position=(0, LAT * t))
                        last.then_inc(lat_done, 1)
                    if s in (4, 7, 10) and soft.exists:
                        values(soft, (s - 4) // 3)

            def wait_for_the_rest():
                pe.wait_ge(router_in, 16 * ROUTER_LOADS)
                pe.wait_ge(gates_made, 1)
                pe.wait_ge(masks_made, 1)
                pe.wait_ge(q_rows_zeroed, 2)
                pe.wait_ge(biases_ready, 1)

            steps(pe, step, after_second=wait_for_the_rest)


_NAMES = ["L0_attn_x", "L0_attn_Wc_down", "L0_attn_Wq_up", "L0_attn_Wkv_up", "L0_attn_Wc_proj", "L0_ffn_w1",
          "L0_ffn_b1", "L0_ffn_w2", "L0_ffn_b2", "L0_ffn_expert_W", "L0_ffn_expert_b", "L0_c", "L0_wmod"]


def kernel(**inputs):
    import numpy as np
    from concourse import bacc
    from concourse.bass_utils import run_bass_kernel_spmd

    nc = bacc.Bacc("TRN2", target_bir_lowering=False, num_devices=1)
    arrays, args = {}, []
    for name in _NAMES:
        a = np.ascontiguousarray(inputs[name])
        arrays[f"in_{name}"] = a
        args.append(nc.dram_tensor(f"in_{name}", a.shape, mybir.dt.from_np(a.dtype), kind="ExternalInput").ap())
    nb, t, c = arrays["in_L0_attn_x"].shape
    hd = arrays["in_L0_attn_Wkv_up"].shape[1] // 2
    out = nc.dram_tensor("out_x", (nb, t, c), F32, kind="ExternalOutput").ap()
    q_scratch = nc.dram_tensor("q_scratch", (2, 3 * hd, c // hd, t), BF16, kind="Internal").ap()
    gate_scratch = nc.dram_tensor("gate_scratch", (nb, 2, c), F32, kind="Internal").ap()
    adaln_block(nc, *args, out, q_scratch, gate_scratch)
    r = run_bass_kernel_spmd(nc, [arrays], core_ids=[0])
    return r.results[0]["out_x"]
```
